# Optimizing a Trainium2 kernel written in Bass

```python
import numpy as np
import jax
import jax.numpy as jnp

def _softmax(x, axis=-1):
    return jax.nn.softmax(x, axis=axis)

def _gelu(x):
    return jax.nn.gelu(x, approximate=True)

def _silu(x):
    return jax.nn.silu(x)

def _sigmoid(x):
    return jax.nn.sigmoid(x)

def _layernorm(x, axis=-1, eps=1e-05):
    m = jnp.mean(x, axis=axis, keepdims=True)
    v = jnp.var(x, axis=axis, keepdims=True)
    return (x - m) / jnp.sqrt(v + eps)

def _scatter_add(tgt, idx, src, axis=0):
    return tgt.at[idx].add(src)

def _segment_sum(src, seg, n):
    return jax.ops.segment_sum(src, seg, n)
kernel_name = 'mk_xattn_seq_d2_seqx_r4_dd33b5'

def setup_inputs(seed: int=0):
    np.random.seed(seed)
    _w = jnp.asarray

    def _rec_inputs():
        import jax
        import jax.numpy as jnp
        _rk = jax.random.key(seed)
        x = 7.22e-05 + 1 * jax.random.normal(jax.random.fold_in(_rk, 1), (64, 128, 256), jnp.float32)
        _lenS = 128 - jax.random.randint(jax.random.fold_in(_rk, 7), (64,), 0, max(1, 128 // 4) + 1, jnp.int32)
        _lenS2 = 128 - jax.random.randint(jax.random.fold_in(_rk, 8), (64,), 0, max(1, 128 // 4) + 1, jnp.int32)
        _ctx_1024P = jax.random.normal(jax.random.fold_in(_rk, 11), (64, 16, 256), jnp.float32)
        _ctx_1024c = jax.random.dirichlet(jax.random.fold_in(_rk, 511), 0.3 * jnp.ones((16,), jnp.float32), (64, 128))
        _ctx_1024t = jnp.einsum('bsk,bkd->bsd', _ctx_1024c, _ctx_1024P)
        _ctx_1024t = _ctx_1024t * jax.lax.rsqrt(jnp.mean(jnp.square(_ctx_1024t)) + 1e-12) * 0.953939
        ctx_1024 = 4.13588e-05 + 0.999923 * (_ctx_1024t + 0.3 * jax.random.normal(jax.random.fold_in(_rk, 611), (64, 128, 256), jnp.float32))
        _validS = jnp.arange(128)[None, :] < _lenS[:, None]
        _validS2 = jnp.arange(128)[None, :] < _lenS2[:, None]
        _causal = jnp.tril(jnp.ones((128, 128), dtype=bool))
        mask_BxS2_ik0 = jnp.where(jnp.broadcast_to(_validS2[:, :], (64, 128)), 0, 1).astype(jnp.int32)
        mask_1xS2_bf0 = jnp.logical_not(jnp.ones((1, 128), dtype=bool))
        return (x, ctx_1024, mask_BxS2_ik0, mask_1xS2_bf0)
    x, ctx_1024, mask_BxS2_ik0, mask_1xS2_bf0 = _rec_inputs()

    def _L0_xattn_setup():
        import jax, jax.numpy as jnp
        import numpy as np
        H = 16
        EPS = 1e-05
        key = jax.random.key(seed)
        ks = jax.random.split(key, 12)
        B, S, D = (4, 512, 256)
        sc = 1.0 / np.sqrt(D)
        return {'queries': jax.random.normal(ks[0], (B, S, D), jnp.float32), 'keys': jax.random.normal(ks[1], (B, S, D), jnp.float32), 'values': jax.random.normal(ks[2], (B, S, D), jnp.float32), 'attention_mask': jax.random.randint(ks[3], (B, S), 0, 2, jnp.int32), 'Wq': jax.random.normal(ks[4], (D, D), jnp.float32) * sc, 'bq': jnp.zeros((D,), jnp.float32), 'Wk': jax.random.normal(ks[5], (D, D), jnp.float32) * sc, 'bk': jnp.zeros((D,), jnp.float32), 'Wv': jax.random.normal(ks[6], (D, D), jnp.float32) * sc, 'bv': jnp.zeros((D,), jnp.float32), 'gamma': jnp.ones((D,), jnp.float32), 'beta': jnp.zeros((D,), jnp.float32)}
    _L0_xattn_all = _L0_xattn_setup()
    _L0_xattn_in = {k: v for k, v in _L0_xattn_all.items() if k in ('Wq', 'bq', 'Wk', 'bk', 'Wv', 'bv', 'gamma', 'beta')}
    del _L0_xattn_all

    def _L1_xattn_setup():
        import jax, jax.numpy as jnp
        import numpy as np
        D = 256
        D_STATE = 128
        N_HEADS = 8
        D_INNER = 2 * D
        HEADDIM = 64
        H_M = D_INNER // HEADDIM
        D_CONV = 4
        CONV_DIM = D_INNER + 2 * D_STATE
        D_IN_PROJ = 2 * D_INNER + 2 * D_STATE + H_M
        B = 1
        LQ = 256
        LK = 512
        EPS = 1e-05

        def _rms(x, w):
            return x * jax.lax.rsqrt(jnp.mean(x * x, axis=-1, keepdims=True) + EPS) * w

        def _ln(x, w, b):
            mu = jnp.mean(x, axis=-1, keepdims=True)
            v = jnp.mean((x - mu) ** 2, axis=-1, keepdims=True)
            return (x - mu) * jax.lax.rsqrt(v + EPS) * w + b

        def _mamba2_block(x, norm_w, in_proj_w, conv_w, conv_b, dt_bias, A_log, D_skip, gnorm_w, out_proj_w):
            b, L, _ = x.shape
            resid = x
            zxbcdt = _rms(x, norm_w) @ in_proj_w
            z = zxbcdt[..., :D_INNER]
            xBC = zxbcdt[..., D_INNER:D_INNER + CONV_DIM]
            dt = jax.nn.softplus(zxbcdt[..., -H_M:] + dt_bias)
            padded = jnp.pad(xBC, ((0, 0), (D_CONV - 1, 0), (0, 0)))
            conv = conv_b + sum((padded[:, k:k + L, :] * conv_w[:, k] for k in range(D_CONV)))
            xBC = jax.nn.silu(conv)
            xh = xBC[..., :D_INNER].reshape(b, L, H_M, HEADDIM)
            Bm = xBC[..., D_INNER:D_INNER + D_STATE]
            Cm = xBC[..., D_INNER + D_STATE:]
            A = -jnp.exp(A_log)
            decay = jnp.exp(dt * A)
            dbx = dt[..., None] * xh

            def step(h, inp):
                dec, u, bt, ct = inp
                h = h * dec[:, :, None, None] + u[..., None] * bt[:, None, None, :]
                y = jnp.einsum('bhpn,bn->bhp', h, ct)
                return (h, y)
            h0 = jnp.zeros((b, H_M, HEADDIM, D_STATE), x.dtype)
            xs = (decay.transpose(1, 0, 2), dbx.transpose(1, 0, 2, 3), Bm.transpose(1, 0, 2), Cm.transpose(1, 0, 2))
            _, ys = jax.lax.scan(step, h0, xs)
            y = ys.transpose(1, 0, 2, 3) + D_skip[None, None, :, None] * xh
            u = _rms(y.reshape(b, L, D_INNER) * jax.nn.silu(z), gnorm_w)
            return resid + u @ out_proj_w

        def _cross_attention(x, enc, pad_mask, ln_w, ln_b, Wq, Wk, Wv, Wo):
            b, Lq, _ = x.shape
            Lk = enc.shape[1]
            dh = D // N_HEADS
            resid = x
            xn = _ln(x, ln_w, ln_b)
            q = (xn @ Wq).reshape(b, Lq, N_HEADS, dh)
            k = (enc @ Wk).reshape(b, Lk, N_HEADS, dh)
            v = (enc @ Wv).reshape(b, Lk, N_HEADS, dh)
            scores = jnp.einsum('bqhd,bkhd->bhqk', q, k) * np.float32(1.0 / np.sqrt(dh))
            scores = jnp.where(pad_mask[:, None, None, :], jnp.float32(-1000000000.0), scores)
            p = jax.nn.softmax(scores, axis=-1)
            ctx = jnp.einsum('bhqk,bkhd->bqhd', p, v).reshape(b, Lq, D)
            return resid + ctx @ Wo
        key = jax.random.key(seed)
        ks = jax.random.split(key, 10)
        s = 0.02
        return {'x': jax.random.normal(ks[0], (B, LQ, D), jnp.float32), 'encoder_out': jax.random.normal(ks[1], (B, LK, D), jnp.float32), 'encoder_padding_mask': jnp.zeros((B, LK), dtype=bool), 'm_norm_w': jnp.ones((D,), jnp.float32), 'in_proj_w': s * jax.random.normal(ks[2], (D, D_IN_PROJ), jnp.float32), 'conv_w': s * jax.random.normal(ks[3], (CONV_DIM, D_CONV), jnp.float32), 'conv_b': jnp.zeros((CONV_DIM,), jnp.float32), 'dt_bias': jnp.full((H_M,), float(np.log(np.expm1(0.01))), jnp.float32), 'A_log': jnp.log(jnp.linspace(1.0, 16.0, H_M)).astype(jnp.float32), 'D_skip': jnp.ones((H_M,), jnp.float32), 'gnorm_w': jnp.ones((D_INNER,), jnp.float32), 'out_proj_w': s * jax.random.normal(ks[4], (D_INNER, D), jnp.float32), 'ca_ln_w': jnp.ones((D,), jnp.float32), 'ca_ln_b': jnp.zeros((D,), jnp.float32), 'Wq': s * jax.random.normal(ks[5], (D, D), jnp.float32), 'Wk': s * jax.random.normal(ks[6], (D, D), jnp.float32), 'Wv': s * jax.random.normal(ks[7], (D, D), jnp.float32), 'Wo': s * jax.random.normal(ks[8], (D, D), jnp.float32)}
    _L1_xattn_all = _L1_xattn_setup()
    _L1_xattn_in = {k: v for k, v in _L1_xattn_all.items() if k in ('m_norm_w', 'in_proj_w', 'conv_w', 'conv_b', 'dt_bias', 'A_log', 'D_skip', 'gnorm_w', 'out_proj_w', 'ca_ln_w', 'ca_ln_b', 'Wq', 'Wk', 'Wv', 'Wo')}
    del _L1_xattn_all
    return {'x': x, 'ctx_1024': ctx_1024, 'mask_BxS2_ik0': mask_BxS2_ik0, 'mask_1xS2_bf0': mask_1xS2_bf0, 'L0_xattn_Wq': _L0_xattn_in['Wq'], 'L0_xattn_bq': _L0_xattn_in['bq'], 'L0_xattn_Wk': _L0_xattn_in['Wk'], 'L0_xattn_bk': _L0_xattn_in['bk'], 'L0_xattn_Wv': _L0_xattn_in['Wv'], 'L0_xattn_bv': _L0_xattn_in['bv'], 'L0_xattn_gamma': _L0_xattn_in['gamma'], 'L0_xattn_beta': _L0_xattn_in['beta'], 'L1_xattn_m_norm_w': _L1_xattn_in['m_norm_w'], 'L1_xattn_in_proj_w': _L1_xattn_in['in_proj_w'], 'L1_xattn_conv_w': _L1_xattn_in['conv_w'], 'L1_xattn_conv_b': _L1_xattn_in['conv_b'], 'L1_xattn_dt_bias': _L1_xattn_in['dt_bias'], 'L1_xattn_A_log': _L1_xattn_in['A_log'], 'L1_xattn_D_skip': _L1_xattn_in['D_skip'], 'L1_xattn_gnorm_w': _L1_xattn_in['gnorm_w'], 'L1_xattn_out_proj_w': _L1_xattn_in['out_proj_w'], 'L1_xattn_ca_ln_w': _L1_xattn_in['ca_ln_w'], 'L1_xattn_ca_ln_b': _L1_xattn_in['ca_ln_b'], 'L1_xattn_Wq': _L1_xattn_in['Wq'], 'L1_xattn_Wk': _L1_xattn_in['Wk'], 'L1_xattn_Wv': _L1_xattn_in['Wv'], 'L1_xattn_Wo': _L1_xattn_in['Wo']}

def reference(x, ctx_1024, mask_BxS2_ik0, mask_1xS2_bf0, L0_xattn_Wq, L0_xattn_bq, L0_xattn_Wk, L0_xattn_bk, L0_xattn_Wv, L0_xattn_bv, L0_xattn_gamma, L0_xattn_beta, L1_xattn_m_norm_w, L1_xattn_in_proj_w, L1_xattn_conv_w, L1_xattn_conv_b, L1_xattn_dt_bias, L1_xattn_A_log, L1_xattn_D_skip, L1_xattn_gnorm_w, L1_xattn_out_proj_w, L1_xattn_ca_ln_w, L1_xattn_ca_ln_b, L1_xattn_Wq, L1_xattn_Wk, L1_xattn_Wv, L1_xattn_Wo):
    import jax
    import jax.numpy as jnp

    def _L0_xattn_ref(queries, keys, values, attention_mask, Wq, bq, Wk, bk, Wv, bv, gamma, beta):
        import jax, jax.numpy as jnp
        import numpy as np
        H = 16
        EPS = 1e-05
        B, S, D = queries.shape
        dh = D // H
        q = jax.nn.relu(jnp.einsum('bsd,de->bse', queries, Wq) + bq)
        k = jax.nn.relu(jnp.einsum('bsd,de->bse', keys, Wk) + bk)
        v = jax.nn.relu(jnp.einsum('bsd,de->bse', values, Wv) + bv)
        q_ = q.reshape(B, S, H, dh).transpose(0, 2, 1, 3)
        k_ = k.reshape(B, S, H, dh).transpose(0, 2, 1, 3)
        v_ = v.reshape(B, S, H, dh).transpose(0, 2, 1, 3)
        scores = jnp.einsum('bhqd,bhkd->bhqk', q_, k_) / jnp.sqrt(jnp.float32(dh))
        m = attention_mask[:, None, :, None].astype(bool)
        scores = jnp.where(m, scores, jnp.float32(1e-09))
        a = jax.nn.softmax(scores, axis=-1)
        o = jnp.einsum('bhqk,bhkd->bhqd', a, v_)
        o = o.transpose(0, 2, 1, 3).reshape(B, S, D)
        x = o + queries
        mu = jnp.mean(x, axis=-1, keepdims=True)
        var = jnp.mean(jnp.square(x - mu), axis=-1, keepdims=True)
        return (x - mu) * jax.lax.rsqrt(var + EPS) * gamma + beta

    def _L1_xattn_ref(x, encoder_out, encoder_padding_mask, m_norm_w, in_proj_w, conv_w, conv_b, dt_bias, A_log, D_skip, gnorm_w, out_proj_w, ca_ln_w, ca_ln_b, Wq, Wk, Wv, Wo):
        import jax, jax.numpy as jnp
        import numpy as np
        D = 256
        D_STATE = 128
        N_HEADS = 8
        D_INNER = 2 * D
        HEADDIM = 64
        H_M = D_INNER // HEADDIM
        D_CONV = 4
        CONV_DIM = D_INNER + 2 * D_STATE
        D_IN_PROJ = 2 * D_INNER + 2 * D_STATE + H_M
        B = 1
        LQ = 256
        LK = 512
        EPS = 1e-05

        def _rms(x, w):
            return x * jax.lax.rsqrt(jnp.mean(x * x, axis=-1, keepdims=True) + EPS) * w

        def _ln(x, w, b):
            mu = jnp.mean(x, axis=-1, keepdims=True)
            v = jnp.mean((x - mu) ** 2, axis=-1, keepdims=True)
            return (x - mu) * jax.lax.rsqrt(v + EPS) * w + b

        def _mamba2_block(x, norm_w, in_proj_w, conv_w, conv_b, dt_bias, A_log, D_skip, gnorm_w, out_proj_w):
            b, L, _ = x.shape
            resid = x
            zxbcdt = _rms(x, norm_w) @ in_proj_w
            z = zxbcdt[..., :D_INNER]
            xBC = zxbcdt[..., D_INNER:D_INNER + CONV_DIM]
            dt = jax.nn.softplus(zxbcdt[..., -H_M:] + dt_bias)
            padded = jnp.pad(xBC, ((0, 0), (D_CONV - 1, 0), (0, 0)))
            conv = conv_b + sum((padded[:, k:k + L, :] * conv_w[:, k] for k in range(D_CONV)))
            xBC = jax.nn.silu(conv)
            xh = xBC[..., :D_INNER].reshape(b, L, H_M, HEADDIM)
            Bm = xBC[..., D_INNER:D_INNER + D_STATE]
            Cm = xBC[..., D_INNER + D_STATE:]
            A = -jnp.exp(A_log)
            decay = jnp.exp(dt * A)
            dbx = dt[..., None] * xh

            def step(h, inp):
                dec, u, bt, ct = inp
                h = h * dec[:, :, None, None] + u[..., None] * bt[:, None, None, :]
                y = jnp.einsum('bhpn,bn->bhp', h, ct)
                return (h, y)
            h0 = jnp.zeros((b, H_M, HEADDIM, D_STATE), x.dtype)
            xs = (decay.transpose(1, 0, 2), dbx.transpose(1, 0, 2, 3), Bm.transpose(1, 0, 2), Cm.transpose(1, 0, 2))
            _, ys = jax.lax.scan(step, h0, xs)
            y = ys.transpose(1, 0, 2, 3) + D_skip[None, None, :, None] * xh
            u = _rms(y.reshape(b, L, D_INNER) * jax.nn.silu(z), gnorm_w)
            return resid + u @ out_proj_w

        def _cross_attention(x, enc, pad_mask, ln_w, ln_b, Wq, Wk, Wv, Wo):
            b, Lq, _ = x.shape
            Lk = enc.shape[1]
            dh = D // N_HEADS
            resid = x
            xn = _ln(x, ln_w, ln_b)
            q = (xn @ Wq).reshape(b, Lq, N_HEADS, dh)
            k = (enc @ Wk).reshape(b, Lk, N_HEADS, dh)
            v = (enc @ Wv).reshape(b, Lk, N_HEADS, dh)
            scores = jnp.einsum('bqhd,bkhd->bhqk', q, k) * np.float32(1.0 / np.sqrt(dh))
            scores = jnp.where(pad_mask[:, None, None, :], jnp.float32(-1000000000.0), scores)
            p = jax.nn.softmax(scores, axis=-1)
            ctx = jnp.einsum('bhqk,bkhd->bqhd', p, v).reshape(b, Lq, D)
            return resid + ctx @ Wo
        h = _mamba2_block(x, m_norm_w, in_proj_w, conv_w, conv_b, dt_bias, A_log, D_skip, gnorm_w, out_proj_w)
        return _cross_attention(h, encoder_out, encoder_padding_mask, ca_ln_w, ca_ln_b, Wq, Wk, Wv, Wo)
    x = _L0_xattn_ref(x, ctx_1024, ctx_1024, mask_BxS2_ik0, L0_xattn_Wq, L0_xattn_bq, L0_xattn_Wk, L0_xattn_bk, L0_xattn_Wv, L0_xattn_bv, L0_xattn_gamma, L0_xattn_beta)
    x = _L1_xattn_ref(x, ctx_1024, mask_1xS2_bf0, L1_xattn_m_norm_w, L1_xattn_in_proj_w, L1_xattn_conv_w, L1_xattn_conv_b, L1_xattn_dt_bias, L1_xattn_A_log, L1_xattn_D_skip, L1_xattn_gnorm_w, L1_xattn_out_proj_w, L1_xattn_ca_ln_w, L1_xattn_ca_ln_b, L1_xattn_Wq, L1_xattn_Wk, L1_xattn_Wv, L1_xattn_Wo)
    return x

_drawn_inputs = setup_inputs


def setup_inputs(seed=0):
    import zlib

    import numpy as np

    out = dict(_drawn_inputs(seed))
    spreads = {'L0_xattn_bq': (0.0, 0.8),
     'L0_xattn_bk': (0.0, 0.8),
     'L0_xattn_bv': (0.0, 0.1),
     'L0_xattn_gamma': (1.0, 0.2),
     'L0_xattn_beta': (0.0, 0.1),
     'L1_xattn_m_norm_w': (1.0, 0.2),
     'L1_xattn_conv_b': (0.0, 0.1),
     'L1_xattn_dt_bias': (-4.600165843963623, 0.6),
     'L1_xattn_D_skip': (1.0, 0.2),
     'L1_xattn_gnorm_w': (1.0, 0.2),
     'L1_xattn_ca_ln_w': (1.0, 0.6),
     'L1_xattn_ca_ln_b': (0.0, 0.8)}
    factors = {'L0_xattn_Wq': 3.491,
     'L0_xattn_Wk': 2.995,
     'L1_xattn_A_log': 8.0,
     'L1_xattn_Wq': 8.0,
     'L1_xattn_Wk': 8.0}
    for name, (base, spread) in spreads.items():
        noise = np.random.default_rng([zlib.crc32(name.encode()), seed]).standard_normal(out[name].shape)
        drawn = base * np.exp(spread * noise) if base else spread * noise
        out[name] = jnp.asarray(drawn.astype(out[name].dtype))
    for name, factor in factors.items():
        out[name] = (out[name] * factor).astype(out[name].dtype)
    return out
```

```python
from contextlib import ExitStack

import concourse.bass as bass
from concourse import mybir

F32 = mybir.dt.float32
BF16 = mybir.dt.bfloat16
ALU = mybir.AluOpType
ACT = mybir.ActivationFunctionType
AX_X = mybir.AxisListType.X

NG = 32
NB = 2
S = 128
D = 256
T = NB * S
EPS = 1e-5
LT = 3
LA = 2
BIG = 3.0e38
NPROJ = 1288


class Engine:

    def __init__(self, sem):
        self.sem, self.n, self.q, self.met = sem, 0, [], {}

    def wait(self, tokens):
        for sem, value in tokens:
            if self.met.get(id(sem), 0) < value:
                self.met[id(sem)] = value
                self.q.append(lambda e, s=sem, v=value: e.wait_ge(s, v))

    def op(self, fn, *tokens, last=True):
        self.wait(tokens)
        if not last:
            self.q.append(fn)
            return None
        self.n += 1
        self.q.append(lambda e: fn(e).then_inc(self.sem, 1))
        return (self.sem, self.n)

    def run(self, e):
        for f in self.q:
            f(e)


class Banks:

    def __init__(self, tiles):
        self.idle = [(t, None) for t in tiles]

    def take(self):
        tile, token = self.idle.pop(0)
        return tile, ([token] if token else [])

    def give(self, tile, token):
        self.idle.append((tile, token))


class Slots:

    def __init__(self, tiles):
        self.tiles, self.free = tiles, [[] for _ in tiles]

    def __getitem__(self, i):
        return self.tiles[i % len(self.tiles)]

    def readers(self, i):
        return self.free[i % len(self.tiles)]

    def read_by(self, i, tokens):
        self.free[i % len(self.tiles)] = list(tokens)


def merge(streams, weights):
    done = [0] * len(streams)
    live = [s is not None for s in streams]
    while any(live):
        i = min((k for k in range(len(streams)) if live[k]), key=lambda k: (done[k] + 0.5) / weights[k])
        try:
            next(streams[i])
            done[i] += 1
        except StopIteration:
            live[i] = False
    return done


def program(nc, a):
    with ExitStack() as ctx:
        def sb(name, shape, dt=F32):
            return ctx.enter_context(nc.sbuf_tensor(name, shape, dt))

        def sem(name):
            return ctx.enter_context(nc.semaphore(name))

        def slots(name, n, shape, dt=F32):
            return Slots([sb(f"{name}{i}", shape, dt) for i in range(n)])

        PE, DV, AC, GP, SP = (Engine(sem(f"s_{n}")) for n in ("pe", "dve", "act", "pool", "sp"))
        banks = Banks([ctx.enter_context(nc.psum_tensor(f"bank{i}", [128, 512], F32)) for i in range(8)])
        dma_sems = {}

        def dma(name, out, in_, *tokens):
            if name not in dma_sems:
                dma_sems[name] = [sem("d_" + name), 0]
            rec = dma_sems[name]
            SP.wait(tokens)
            if rec[1]:
                SP.wait([(rec[0], rec[1])])
            rec[1] += 16
            SP.q.append(lambda e, s=rec[0]: e.dma_start(out, in_).then_inc(s, 16))
            return (rec[0], rec[1])

        ident = sb("ident", [128, 128])
        id8 = sb("id8", [128, 8, 128])
        par = sb("par", [128, 2])
        sel = sb("sel", [128, 3])
        onesb = sb("onesb", [128, 128], BF16)
        wq = sb("wq", [128, 2, 256])
        wk = sb("wk", [128, 2, 256])
        wv = sb("wv", [128, 2, 512])
        wk1 = sb("wk1", [128, 2, 256])
        wq1 = sb("wq1", [128, 2, 256])
        wo = sb("wo", [128, 2, 256])
        win = sb("win", [128, 2, NPROJ])
        wout = sb("wout", [128, 4, 256])
        pc = sb("pc", [128, 20])
        cw = sb("cw", [128, 6, 5])
        gam = sb("gam", [128, 256])
        bet = sb("bet", [128, 256])
        h8 = sb("h8", [128, 3, 8])
        negA = sb("negA", [128, 8])
        mrow = sb("mrow", [128, 128], mybir.dt.uint8)
        mi = sb("mi", [128, 64], mybir.dt.int32)
        sq = sb("sq", [128, 64])
        keep = sb("keep", [128, 128])
        negm = sb("negm", [128, 128])
        maskb = sb("maskb", [128, 4, 128], BF16)
        bvr = sb("bvr", [128, 256])
        vbias = sb("vbias", [128, 512], BF16)
        mhalf = sb("mhalf", [128, 1])
        kb = sb("kb", [128, 2, 2])
        bq1 = sb("bq1", [128, 2])

        xT = slots("xT", 1, [128, 2, T])
        cT = slots("cT", 1, [128, 2, T])
        xt = slots("xt", 2, [128, NB, D])
        QT = slots("QT", 2, [128, 2, T])
        KT = slots("KT", 2, [128, 2, NB, 2, 128])
        V0 = slots("V0", 2, [128, NB, 16, 17])
        K1T = slots("K1T", 6, [128, 2, T])
        V1 = slots("V1", 6, [128, NB, 8, 33])
        PA = slots("PA", LT + 1, [128, 4, 128])
        PTA = slots("PTA", LA + 1, [128, 4, 128])
        PC_ = slots("PC", LT + 1, [128, 4, 128])
        PTC = slots("PTC", LA + 1, [128, 4, 128])
        X2 = slots("X2", 5, [128, NB, D])
        sta = slots("sta", 4, [128, 48])
        stb = slots("stb", 4, [128, 16])
        stn = slots("stn", 4, [128, 1])
        stc = slots("stc", 4, [128, 32])
        xa = slots("xa", 2, [128, 256])
        xn = slots("xn", 2, [128, 256])
        xnT = slots("xnT", 2, [128, 2, T])
        XP = slots("XP", 3, [128, NB, 131])
        ACC = slots("ACC", 4, [128, NB, 128])
        XC = slots("XC", 2, [128, 6, T])
        SZ = slots("SZ", 2, [128, 512])
        dts = sb("dts", [128, 8, 8 * NB])
        dtt = slots("dtt", 3, [128, 8 * NB])
        decT = slots("decT", 2, [8 * NB, 128])
        DB = slots("DB", 2, [128, 1024])
        L = slots("L", 2, [128, 8, 128])
        XH = slots("XH", 1, [128, 512])
        DX = slots("DX", 2, [128, 512])
        Y = slots("Y", 2, [128, 512])
        UT = slots("UT", 2, [128, 4, 128])
        xh = slots("xh", 2, [128, 256])
        HT = slots("HT", 2, [128, 2, T])
        Q1T = slots("Q1T", 2, [128, 2, T])
        oc = slots("oc", 2, [128, 256])
        OT = slots("OT", 1, [128, 2, 128])
        res = slots("res", 2, [128, 256])
        junk = sb("junk", [128, 512], BF16)
        scratch = nc.dram_tensor("dec_scratch", [NG, NB * 8 * 128], F32, kind="Internal").ap()

        s0, s1, s2 = UT[0][:, 0:2, :], UT[0][:, 2, :].bitcast(BF16), Y[0][:, 0:256]
        s0 = s0.rearrange("p a b -> p (a b)")

        def bcast(v, n):
            return v.rearrange("(a n) -> a n", a=1).to_broadcast([128, n])

        consts = dma("c_id", ident[:, :], a["ident"])
        t_sel = dma("c_sel", sel[:, :], a["sel"])
        t_par = dma("c_par", par[:, :], a["par"])
        t_pc = dma("c_pc", pc[:, :], a["pcols"])
        t_cw = dma("c_cw", cw[:, :, :], a["convp"])
        t_mi = dma("c_mi", mi[:, :], a["maskT"])
        t_w = [dma("w_" + n, t[:, :, :], a[n]) for n, t in
               (("wq", wq), ("wk", wk), ("wv", wv), ("wk1", wk1))]

        loads = {}

        def load(name, ring, g):
            if g < NG:
                loads[name, g] = dma(f"{name}{g % len(ring.tiles)}", ring[g][:, :, :], a[name][g], *ring.readers(g))

        load("xT", xT, 0)
        load("cT", cT, 0)
        load("xt", xt, 0)
        t_h8 = dma("c_h8", h8[:, :, :], a["heads"].rearrange("a (b c) -> a b c", b=3).to_broadcast([128, 3, 8]))
        t_bv = dma("c_bv", bvr[:, :], bcast(a["bv"], 256))
        t_mr = dma("c_mr", mrow[:, :], a["pad"].to_broadcast([128, 128]))
        t_gam = dma("c_gam", gam[:, :], bcast(a["gamma"], 256))
        t_bet = dma("c_bet", bet[:, :], bcast(a["beta"], 256))
        t_win = dma("w_win", win[:, :, :], a["win"])
        t_wout = dma("w_wout", wout[:, :, :], a["wout"])
        t_wq1 = dma("w_wq1", wq1[:, :, :], a["wq1"])
        t_wo = dma("w_wo", wo[:, :, :], a["wo"])

        t_ones = GP.op(lambda e: e.memset(onesb[:, :], 1.0))
        t_mh = GP.op(lambda e: e.memset(mhalf[:, :], -0.5))
        t_pad = []
        for i in range(3):
            t_pad.append(GP.op(lambda e, i=i: e.memset(XP[i][:, :, 0:3], 0.0)))
        for i in range(2):
            t_pad.append(GP.op(lambda e, i=i: e.memset(decT[i][:, 0:1], 0.0)))
            t_pad.append(GP.op(lambda e, i=i: e.memset(V0[i][:, :, :, 16:17], 1.0)))
        for i in range(6):
            t_pad.append(GP.op(lambda e, i=i: e.memset(V1[i][:, :, :, 32:33], 1.0)))
        t_id8 = [GP.op(lambda e, h=h: e.tensor_copy(id8[:, h, :], ident[:, :]), consts) for h in range(8)][-1]
        t_sq = DV.op(lambda e: e.tensor_scalar(sq[:, :], mi[:, :], 0.0, 0.25, ALU.not_equal, ALU.mult), t_mi)
        t_kb = DV.op(lambda e: e.tensor_scalar(kb[:, 0, :], pc[:, 2:4], par[:, 0:1], None, ALU.mult), t_pc, t_par)
        t_k1 = DV.op(lambda e: e.tensor_scalar(s0[:, 0:1], par[:, 0:1], -BIG, None, ALU.mult), t_par)
        t_kb1 = DV.op(lambda e: e.tensor_scalar(kb[:, 1, :], pc[:, 2:4], s0[:, 0:1], None, ALU.add), t_k1)
        t_keep = DV.op(lambda e: e.tensor_scalar(keep[:, :], mrow[:, :], 0.0, None, ALU.is_equal), t_mr)
        t_neg = DV.op(lambda e: e.tensor_scalar(negm[:, :], mrow[:, :], 0.0, -1.0e9 * 32 ** 0.5,
                                                ALU.not_equal, ALU.mult), t_mr)

        def split3(src, n, dst, token):
            t = DV.op(lambda e: e.tensor_copy(s1[:, 0:n], src), token, t_sel)
            p = DV.op(lambda e: e.tensor_scalar(s0[:, 0:n], s1[:, 0:n], sel[:, 0:1], None, ALU.mult), t)
            r = DV.op(lambda e: e.tensor_tensor(s2[:, 0:n], src, s1[:, 0:n], ALU.subtract), t)
            for i in (1, 2):
                t = DV.op(lambda e: e.tensor_copy(s1[:, 0:n], s2[:, 0:n]), r, p)
                p = DV.op(lambda e, i=i: e.scalar_tensor_tensor(out=s0[:, 0:n], in0=s1[:, 0:n], scalar=sel[:, i:i + 1],
                                                                in1=s0[:, 0:n], op0=ALU.mult, op1=ALU.add), t, p)
                r = DV.op(lambda e: e.tensor_tensor(s2[:, 0:n], s2[:, 0:n], s1[:, 0:n], ALU.subtract), t)
            return DV.op(lambda e: e.tensor_copy(dst, s0[:, 0:n]), p, r)

        t_vb0 = DV.op(lambda e: e.memset(vbias[:, 256:512], 0.0))
        t_vb = split3(bvr[:, :], 256, vbias[:, 0:256], t_bv)
        t_mb = split3(negm[:, :], 128, maskb[:, 0, :], t_neg)
        for i in range(1, 4):
            t_mb = DV.op(lambda e, i=i: e.tensor_copy(maskb[:, i, :], maskb[:, 0, :]), t_mb)
        for k in range(2):
            ins = ((0, 512, 0.5), (512, NPROJ, 1.0))
            for lo, hi, c in ins:
                t_wz = GP.op(lambda e, k=k, lo=lo, hi=hi, c=c: e.tensor_scalar(
                    win[:, k, lo:hi], win[:, k, lo:hi], pc[:, 4 + k:5 + k], c, ALU.mult, ALU.mult), t_win, t_pc)
        for k in range(4):
            t_wo2 = GP.op(lambda e, k=k: e.tensor_scalar(
                wout[:, k, :], wout[:, k, :], pc[:, 6 + k:7 + k], None, ALU.mult), t_wout, t_pc)
        t_cw2 = GP.op(lambda e: e.tensor_scalar(cw[:, :, :], cw[:, :, :], 0.5, None, ALU.mult), t_cw)
        bk, w = banks.take()
        for m in range(2):
            for k in range(2):
                t_b1 = PE.op(lambda e, m=m, k=k: e.matmul(bk[:, m:m + 1], wq1[:, k, m * 128:(m + 1) * 128],
                                                          pc[:, 12 + k:13 + k], start=(k == 0), stop=(k == 1)),
                             t_wq1, t_pc, *w)
        t_bq1 = DV.op(lambda e: e.tensor_copy(bq1[:, :], bk[:, 0:2]), t_b1)
        banks.give(bk, t_bq1)
        for k in range(2):
            t_wq1s = GP.op(lambda e, k=k: e.tensor_scalar(wq1[:, k, :], wq1[:, k, :], pc[:, 10 + k:11 + k], None,
                                                          ALU.mult), t_b1)
        t_ea = AC.op(lambda e: e.activation(negA[:, :], h8[:, 1, :], ACT.Exp), t_h8)
        t_nA = DV.op(lambda e: e.tensor_scalar(negA[:, :], negA[:, :], -1.0, None, ALU.mult), t_ea)

        tok = {}

        def project(w_ap, src, m, *tokens):
            bk, free = banks.take()
            for k in range(2):
                t = PE.op(lambda e, k=k: e.matmul(bk[:, 0:T], w_ap[:, k, m * 128:(m + 1) * 128], src[:, k, :],
                                                  start=(k == 0), stop=(k == 1)), *tokens, *free, last=(k == 1))
            return bk, t

        def turns(bk, src, col, n, *tokens, last=True):
            for i in range(n):
                t = PE.op(lambda e, i=i: e.transpose(bk[:, col + i * 128:col + (i + 1) * 128], src(i), ident[:, :]),
                          *tokens, consts, last=(last and i == n - 1))
            return t

        def softmax_part(bk, t_s, ring, n, st, scale, tokens, mcol):
            P = ring[n]
            v = bk[:, :].rearrange("p (i k) -> p i k", i=4)
            mx = st[:, mcol:mcol + 4]
            t_m = DV.op(lambda e: e.tensor_reduce(mx, v, AX_X, ALU.max), t_s, *tokens)
            t_d = DV.op(lambda e: e.tensor_tensor(P[:, :, :], v, mx.unsqueeze(2).to_broadcast([128, 4, 128]),
                                                  ALU.subtract), t_m, *ring.readers(n))
            banks.give(bk, t_d)
            return lambda: AC.op(lambda e: e.activation(P[:, :, :], P[:, :, :], ACT.Exp, scale=scale), t_d)

        def layer_stats(src, st, c, token, *more):
            t = DV.op(lambda e: e.bn_stats(st[:, c + 2:c + 8], src), token, *more)
            t = DV.op(lambda e: e.bn_aggr(st[:, c:c + 2], st[:, c + 2:c + 8]), t)
            t = GP.op(lambda e: e.tensor_scalar(st[:, c + 1:c + 2], st[:, c + 1:c + 2], EPS, None, ALU.add), t)
            return GP.op(lambda e: e.tensor_tensor(st[:, c + 1:c + 2], st[:, c + 1:c + 2], mhalf[:, :], ALU.pow), t, t_mh)

        qa = [0]

        def stream_a1(g):
            t_x, t_c = (loads[n, g] for n in ("xT", "cT"))
            readers_q, readers_k = [], []
            for m in range(2):
                bk, t = project(wq, xT[g], m, t_x, t_w[0])
                t_q = AC.op(lambda e, m=m, bk=bk: e.activation(QT[g][:, m, :], bk[:, 0:T], ACT.Relu, bias=pc[:, m:m + 1]),
                            t, t_pc, *QT.readers(g))
                banks.give(bk, t_q)
                yield
            xT.read_by(g, [t])
            load("xT", xT, g + 1)
            for m in range(2):
                bk, t = project(wk, cT[g], m, t_c, t_w[1])
                v = bk[:, 0:T].rearrange("p (b k) -> p b k", b=NB)
                t_k = AC.op(lambda e, m=m, v=v: e.activation(KT[g][:, m, :, 0, :], v, ACT.Relu, bias=kb[:, 0, m:m + 1],
                                                             scale=par[:, 0:1]), t, t_kb, t_par, *KT.readers(g))
                t_k2 = DV.op(lambda e, m=m, v=v: e.tensor_scalar(KT[g][:, m, :, 1, :], v, kb[:, 1, m:m + 1], 0.0,
                                                                 ALU.add, ALU.max), t_k, t_kb1, *KT.readers(g))
                banks.give(bk, t_k2)
                yield
            for m in range(2):
                bk, t = project(wk1, cT[g], m, t_c, t_w[3])
                v = bk[:, 0:T].rearrange("p (b k) -> p b k", b=NB)
                t_k1 = DV.op(lambda e, m=m, v=v: e.tensor_tensor(
                    K1T[g][:, m, :].rearrange("p (b k) -> p b k", b=NB), v,
                    keep[:, :].unsqueeze(1).to_broadcast([128, NB, 128]), ALU.mult), t, t_keep, *K1T.readers(g))
                banks.give(bk, t_k1)
                yield
            t_v = []
            for b in range(NB):
                bk, free = banks.take()
                PE.op(lambda e, bk=bk: e.matmul(bk[:, :], onesb[0:3, :], vbias[0:3, :], start=True, stop=False),
                      t_ones, t_vb, t_vb0, *free, last=False)
                for k in range(2):
                    t = PE.op(lambda e, bk=bk, k=k, b=b: e.matmul(bk[:, :], cT[g][:, k, b * 128:(b + 1) * 128],
                                                                  wv[:, k, :], start=False, stop=(k == 1)), t_w[2],
                              last=(k == 1))
                AC.op(lambda e, bk=bk, b=b: e.activation(
                    V0[g][:, b, :, 0:16], bk[:, 0:256].rearrange("p (h d) -> p h d", h=16), ACT.Relu),
                    t, *t_pad, *V0.readers(g))
                t_v.append(AC.op(lambda e, bk=bk, b=b: e.activation(
                    V1[g][:, b, :, 0:32], bk[:, 256:512].rearrange("p (h d) -> p h d", h=8), ACT.Copy),
                    t, *V1.readers(g)))
                banks.give(bk, t_v[-1])
                yield
            cT.read_by(g, [t])
            load("cT", cT, g + 1)
            tok["ctx", g] = (t_k1, t_v)
            tok["qkv", g] = (t_q, t_k, t_k2, t_v)

        def stream_a2(g):
            t_q, t_k, t_k2, t_v = tok["qkv", g]
            t_xt = loads["xt", g]
            load("xt", xt, g + 1)

            units = [(b, j) for b in range(NB) for j in range(4)]
            exp_t, pt_t, av = {}, {}, {}
            N = len(units)
            t_last = None
            for i in range(N + LT + LA):
                if i < N:
                    b, j = units[i]
                    n = qa[0] + i
                    bk, free = banks.take()
                    r = slice(32 * j, 32 * j + 32)
                    for m in range(2):
                        t_s = PE.op(lambda e, bk=bk, m=m, b=b, r=r: e.matmul(
                            bk[:, m * 256:(m + 1) * 256], QT[g][r, m, b * 128:(b + 1) * 128], KT[g][r, m, b, :, :],
                            start=True, stop=True), t_q, t_k, t_k2, *free, last=(m == 1))
                    ns = g * NB + b
                    late_exp = softmax_part(bk, t_s, PA, n, sta[ns], sq[:, ns:ns + 1],
                                            [t_sq, *(sta.readers(ns) if j == 0 else [])], 4 * j)
                    yield
                if LT <= i < N + LT:
                    b, j = units[i - LT]
                    n = qa[0] + i - LT
                    bk, free = banks.take()
                    P = PA[n]
                    t = turns(bk, lambda q, P=P: P[:, q, :], 0, 4, exp_t[i - LT], *free)
                    PA.read_by(n, [t])
                    t = AC.op(lambda e, bk=bk, n=n: e.activation(PTA[n][:, :, :], bk[:, :].rearrange(
                        "p (i k) -> p i k", i=4), ACT.Copy), t, *PTA.readers(n))
                    banks.give(bk, t)
                    pt_t[i - LT] = t
                    yield
                if i < N:
                    exp_t[i] = late_exp()
                if LT + LA <= i:
                    b, j = units[i - LT - LA]
                    n = qa[0] + i - LT - LA
                    if j == 0:
                        av[b] = banks.take()
                    o, free = av[b]
                    for q in range(4):
                        hd = (q // 2) * 8 + 2 * j + q % 2
                        t = PE.op(lambda e, o=o, n=n, q=q, b=b, hd=hd: e.matmul(
                            o[:, hd * 17:hd * 17 + 17], PTA[n][:, q, :], V0[g][:, b, hd, :], start=True, stop=True),
                            pt_t[i - LT - LA], t_v[b], *free, last=(q == 3))
                    PTA.read_by(n, [t])
                    t_last = t
                    if j == 3:
                        yield
                        ns = g * NB + b
                        st = sta[ns]
                        ov = o[:, 0:272].rearrange("p (h d) -> p h d", h=16)
                        xv = xa[ns][:, :].rearrange("p (h d) -> p h d", h=16)
                        t = DV.op(lambda e, st=st, ov=ov: e.reciprocal(st[:, 16:32].unsqueeze(2), ov[:, :, 16:17]), t)
                        t = DV.op(lambda e, st=st, ov=ov, xv=xv: e.tensor_tensor(
                            xv, ov[:, :, 0:16], st[:, 16:32].unsqueeze(2).to_broadcast([128, 16, 16]), ALU.mult),
                            t, *xa.readers(ns))
                        banks.give(o, t)
                        t = GP.op(lambda e, ns=ns, b=b: e.tensor_tensor(xa[ns][:, :], xa[ns][:, :], xt[g][:, b, :],
                                                                        ALU.add), t, t_xt)
                        t_xr = t
                        yield
                        t = layer_stats(xa[ns][:, :], st, 32, t)
                        x2 = X2[g][:, b, :]
                        t = DV.op(lambda e, ns=ns, st=st: e.tensor_scalar(
                            xa[ns][:, :], xa[ns][:, :], st[:, 32:33], st[:, 33:34], ALU.subtract, ALU.mult), t)
                        sta.read_by(ns, [t])
                        yield
                        t = GP.op(lambda e, ns=ns, x2=x2: e.tensor_tensor(x2, xa[ns][:, :], gam[:, :], ALU.mult),
                                  t, t_gam, *X2.readers(g))
                        xa.read_by(ns, [t])
                        t = GP.op(lambda e, x2=x2: e.tensor_tensor(x2, x2, bet[:, :], ALU.add), t, t_bet)
                        tok["x2", g, b] = t
                    yield
            QT.read_by(g, [t_s])
            KT.read_by(g, [t_s])
            V0.read_by(g, [t_last])
            xt.read_by(g, [t_xr])
            qa[0] += N

        def stream_b1(g):
            t_r = []
            for b in range(NB):
                ns = g * NB + b
                x2 = X2[g][:, b, :]
                t = AC.op(lambda e, x2=x2, ns=ns: e.activation(junk[:, 0:256], x2, ACT.Square, scale=1.0 / 16,
                                                               accum_out=stn[ns][:, 0:1]),
                          tok["x2", g, b], (AC.sem, AC.n), *stn.readers(ns))
                t = GP.op(lambda e, ns=ns: e.tensor_scalar(stn[ns][:, :], stn[ns][:, :], EPS, None, ALU.add), t)
                t_r.append(GP.op(lambda e, ns=ns: e.tensor_tensor(stn[ns][:, :], stn[ns][:, :], mhalf[:, :], ALU.pow),
                                 t, t_mh))
                yield
            t_n = []
            for b in range(NB):
                ns = g * NB + b
                t = DV.op(lambda e, ns=ns, b=b: e.tensor_scalar(xn[ns][:, :], X2[g][:, b, :], stn[ns][:, 0:1], None,
                                                                ALU.mult), t_r[b], *xn.readers(ns))
                stn.read_by(ns, [t])
                t_n.append(t)
            yield
            yield
            bk, free = banks.take()
            for b in range(NB):
                ns = g * NB + b
                t = turns(bk, lambda i, ns=ns: xn[ns][:, i * 128:(i + 1) * 128], b * 256, 2, t_n[b], *free)
                xn.read_by(ns, [t])
            v = bk[:, :].rearrange("p (b k t) -> p k b t", b=NB, k=2)
            o = xnT[g][:, :, :].rearrange("p k (b t) -> p k b t", b=NB)
            for k in range(2):
                t = AC.op(lambda e, v=v, o=o, k=k: e.activation(o[:, k], v[:, k], ACT.Copy), t, *xnT.readers(g))
            banks.give(bk, t)
            t_n = t
            tok["xnT", g] = t
            yield
            yield

            d = [dts[:, i, :] for i in range(8)]
            dt = dtt[g][:, :]
            v4 = lambda x: x.rearrange("p (b h) -> p b h", b=NB)
            bc = lambda x: x.unsqueeze(1).to_broadcast([128, NB, 8])

            def steps():
                bk, free = banks.take()
                for b in range(NB):
                    for k in range(2):
                        t = PE.op(lambda e, bk=bk, k=k, b=b: e.matmul(
                            bk[:, b * 8:b * 8 + 8], xnT[g][:, k, b * 128:(b + 1) * 128], win[:, k, 1280:1288],
                            start=(k == 0), stop=(k == 1)), t_n, t_wz, *free, last=(b == NB - 1 and k == 1))
                t = DV.op(lambda e: e.tensor_tensor(v4(d[0]), v4(bk[:, 0:8 * NB]), bc(h8[:, 0, :]), ALU.add), t, t_h8,
                          *tok.get("dts", []))
                banks.give(bk, t)
                yield
                t = AC.op(lambda e: e.activation(d[1], d[0], ACT.Abs), t)
                t_e = AC.op(lambda e: e.activation(d[1], d[1], ACT.Exp, scale=-1.0), t)
                yield
                t_w = DV.op(lambda e: e.tensor_scalar(d[2], d[1], 1.0, None, ALU.add), t_e)
                t_w1 = DV.op(lambda e: e.tensor_scalar(d[4], d[2], 1.0, None, ALU.subtract), t_w)
                yield
                t_l = AC.op(lambda e: e.activation(d[3], d[2], ACT.Ln), t_w)
                t = GP.op(lambda e: e.tensor_scalar(d[5], d[4], 0.0, None, ALU.is_equal), t_w1)
                t_g = GP.op(lambda e: e.tensor_tensor(d[5], d[5], d[1], ALU.mult), t)
                yield
                t = DV.op(lambda e: e.tensor_scalar(d[4], d[4], 1e-30, None, ALU.max), t_g)
                t = DV.op(lambda e: e.reciprocal(d[6], d[4]), t)
                t = DV.op(lambda e: e.tensor_tensor(d[6], d[6], d[1], ALU.mult), t)
                t = DV.op(lambda e: e.tensor_tensor(d[6], d[6], d[3], ALU.mult), t, t_l)
                t = DV.op(lambda e: e.tensor_tensor(d[6], d[6], d[5], ALU.add), t)
                t_dt = DV.op(lambda e: e.scalar_tensor_tensor(out=dt, in0=d[0], scalar=0.0, in1=d[6], op0=ALU.max,
                                                              op1=ALU.add), t, *dtt.readers(g))
                tok["dt", g] = t_dt
                t = DV.op(lambda e: e.tensor_tensor(v4(d[7]), v4(dt), bc(negA[:, :]), ALU.mult), t_dt, t_nA)
                yield
                t_a = AC.op(lambda e: e.activation(d[7], d[7], ACT.Exp), t)
                yield
                yield
                bd, free = banks.take()
                t = PE.op(lambda e: e.transpose(bd[0:8 * NB, 0:128], d[7], ident[:, :]), t_a, *free)
                tok["dts"] = [t, t_dt]
                t = DV.op(lambda e: e.tensor_copy(decT[g][:, 1:128], bd[0:8 * NB, 1:128]), t, *decT.readers(g),
                          *t_pad)
                banks.give(bd, t)
                t = dma(f"scr{g % 2}", scratch[g].rearrange("(p t) -> p t", p=8 * NB), decT[g][:, :], t)
                decT.read_by(g, [t])
                tok["scr", g] = t

            ds = steps()
            acc_t = {}
            for i in range(8):
                next(ds, None)
                if i < 6:
                    n, c = g * 6 + i, i
                    bk, t = project(win[:, :, 512:1280], xnT[g], c, t_n, t_wz)
                    v = bk[:, 0:T].rearrange("p (b t) -> p b t", b=NB)
                    t1 = AC.op(lambda e, v=v, n=n: e.activation(XP[n][:, :, 3:131], v, ACT.Copy), t, *t_pad,
                               *XP.readers(n))
                    t2 = AC.op(lambda e, v=v, n=n, c=c: e.activation(
                        ACC[n][:, :, :], v, ACT.Identity, bias=cw[:, c, 4:5], scale=cw[:, c, 3:4]),
                        t, t_cw2, *ACC.readers(n))
                    banks.give(bk, t2)
                    acc_t[i] = t1, t2
                    yield
                if 1 <= i < 7:
                    n, c = g * 6 + i - 1, i - 1
                    t1, t = acc_t[i - 1]
                    for k in range(3):
                        t = DV.op(lambda e, k=k, n=n, c=c: e.scalar_tensor_tensor(
                            out=ACC[n][:, :, :], in0=XP[n][:, :, k:k + 128], scalar=cw[:, c, k:k + 1],
                            in1=ACC[n][:, :, :], op0=ALU.mult, op1=ALU.add), t, t1, t_cw2)
                    XP.read_by(n, [t])
                    acc_t[i - 1] = t
                    yield
                if i >= 2:
                    n, c = g * 6 + i - 2, i - 2
                    xc = XC[g][:, c, :].rearrange("p (b t) -> p b t", b=NB)
                    t = AC.op(lambda e, n=n, xc=xc: e.activation(xc, ACC[n][:, :, :], ACT.Tanh), acc_t[i - 2],
                              *XC.readers(g))
                    yield
                    t_xc = DV.op(lambda e, n=n, xc=xc: e.scalar_tensor_tensor(
                        out=xc, in0=xc, scalar=1.0, in1=ACC[n][:, :, :], op0=ALU.add, op1=ALU.mult), t)
                    ACC.read_by(n, [t_xc])
                    yield
            for _ in ds:
                yield
            tok["xc", g] = t_xc

        t_db = {}

        def fetch(ns):
            g, b = ns // NB, ns % NB
            t_db[ns] = dma(f"db{ns % 2}", DB[ns][:, :], scratch[g, b * 1024:(b + 1) * 1024].rearrange(
                "(a n) -> a n", a=1).to_broadcast([128, 1024]), tok["scr", g], *DB.readers(ns))

        hv = lambda x: x.rearrange("p (h d) -> p h d", h=8)

        def first_half(ns):
            g, b = ns // NB, ns % NB
            t_xc, t_dt = tok["xc", g], tok["dt", g]
            ts = slice(b * 128, (b + 1) * 128)
            if ns not in t_db:
                fetch(ns)
            bx, free = banks.take()
            t_x = turns(bx, lambda i: XC[g][:, i, ts], 0, 4, t_xc, *free)
            t = AC.op(lambda e: e.activation(XH[ns][:, :], bx[:, :], ACT.Copy), t_x, *XH.readers(ns))
            banks.give(bx, t)
            t_dx = GP.op(lambda e: e.tensor_tensor(
                hv(DX[ns][:, :]), hv(XH[ns][:, :]),
                h8[:, 2, :].unsqueeze(2).to_broadcast([128, 8, 64]), ALU.mult), t, *DX.readers(ns))
            t_xd = GP.op(lambda e: e.tensor_tensor(
                hv(XH[ns][:, :]), hv(XH[ns][:, :]),
                dtt[g][:, b * 8:b * 8 + 8].unsqueeze(2).to_broadcast([128, 8, 64]), ALU.mult), t_dx, t_dt)
            t_l = DV.op(lambda e: e.tensor_tensor_scan(
                L[ns][:, :, :].rearrange("p h t -> p (h t)"), DB[ns][:, :],
                id8[:, :, :].rearrange("p h t -> p (h t)"), 0.0, ALU.mult, ALU.add),
                t_db[ns], t_id8, *L.readers(ns))
            DB.read_by(ns, [t_l])
            yield
            bg, free = banks.take()
            t_gm = PE.op(lambda e: e.matmul(bg[:, 0:128], XC[g][:, 4, ts], XC[g][:, 5, ts],
                                            start=True, stop=True), t_xc, *free)
            yield
            t_m = DV.op(lambda e: e.tensor_tensor(
                L[ns][:, :, :], L[ns][:, :, :], bg[:, 0:128].unsqueeze(1).to_broadcast([128, 8, 128]), ALU.mult),
                t_l, t_gm)
            banks.give(bg, t_m)
            if b == NB - 1:
                XC.read_by(g, [t_gm])
            yield
            bz, free = banks.take()
            for k in range(2):
                t_x = PE.op(lambda e, k=k: e.matmul(bz[:, :], xnT[g][:, k, ts], win[:, k, 0:512],
                                                    start=(k == 0), stop=(k == 1)), tok["xnT", g], *free,
                            last=(k == 1))
            if b == NB - 1:
                xnT.read_by(g, [t_x])
            t = AC.op(lambda e: e.activation(SZ[ns][:, :], bz[:, :], ACT.Tanh), t_x, *SZ.readers(ns))
            yield
            t_sz = DV.op(lambda e: e.scalar_tensor_tensor(
                out=SZ[ns][:, :], in0=SZ[ns][:, :], scalar=1.0, in1=bz[:, :], op0=ALU.add, op1=ALU.mult), t)
            banks.give(bz, t_sz)
            yield
            yield
            yield
            by, free = banks.take()
            for h in range(8):
                t = PE.op(lambda e, h=h: e.matmul(
                    by[:, h * 64:h * 64 + 64], L[ns][:, h, :], XH[ns][:, h * 64:h * 64 + 64],
                    start=True, stop=True), t_m, t_xd, *free, last=(h == 7))
            L.read_by(ns, [t])
            XH.read_by(ns, [t])
            dtt.read_by(g, [t_xd])
            if ("scr", (ns + 1) // NB) in tok:
                fetch(ns + 1)
            yield
            t = DV.op(lambda e: e.tensor_tensor(Y[ns][:, :], by[:, :], DX[ns][:, :], ALU.add),
                      t, t_dx, *Y.readers(ns))
            DX.read_by(ns, [t])
            banks.give(by, t)
            t = GP.op(lambda e: e.tensor_tensor(Y[ns][:, :], Y[ns][:, :], SZ[ns][:, :], ALU.mult), t, t_sz)
            SZ.read_by(ns, [t])
            tok["y", ns] = t

        def second_half(ns):
            g, b = ns // NB, ns % NB
            st = stb[ns]
            t_y = tok["y", ns]
            t = t_sqr = AC.op(lambda e: e.activation(junk[:, :], Y[ns][:, :], ACT.Square, accum_out=st[:, 1:2]),
                              t_y, (AC.sem, AC.n), *stb.readers(ns))
            t = GP.op(lambda e: e.tensor_scalar(st[:, 1:2], st[:, 1:2], 1.0 / 512, EPS, ALU.mult, ALU.add), t)
            t_r2 = GP.op(lambda e: e.tensor_tensor(st[:, 1:2], st[:, 1:2], mhalf[:, :], ALU.pow), t)
            bu, free = banks.take()
            t = turns(bu, lambda i: Y[ns][:, i * 128:(i + 1) * 128], 0, 4, t_y, *free)
            Y.read_by(ns, [t, t_sqr])
            t = AC.op(lambda e: e.activation(UT[ns][:, :, :], bu[:, :].rearrange(
                "p (k t) -> p k t", k=4), ACT.Copy), t, *UT.readers(ns))
            banks.give(bu, t)
            yield
            yield
            bo, free = banks.take()
            t_u = t
            for k in range(4):
                t = PE.op(lambda e, k=k: e.matmul(bo[:, 0:256], UT[ns][:, k, :], wout[:, k, :],
                                                  start=(k == 0), stop=(k == 3)), t_u, t_wo2, *free, last=(k == 3))
            UT.read_by(ns, [t])
            hh = X2[g][:, b, :]
            t = DV.op(lambda e: e.scalar_tensor_tensor(
                out=hh, in0=bo[:, 0:256], scalar=st[:, 1:2], in1=X2[g][:, b, :], op0=ALU.mult, op1=ALU.add),
                t, t_r2)
            banks.give(bo, t)
            t = layer_stats(hh, st, 2, t)
            yield
            t = DV.op(lambda e: e.tensor_scalar(
                xh[ns][:, :], hh, st[:, 2:3], st[:, 3:4], ALU.subtract, ALU.mult), t, *xh.readers(ns))
            stb.read_by(ns, [t])
            yield
            yield
            hb, free = banks.take()
            t = turns(hb, lambda i: xh[ns][:, i * 128:(i + 1) * 128], 0, 2, t, *free)
            xh.read_by(ns, [t])
            t = AC.op(lambda e: e.activation(HT[g][:, :, b * 128:(b + 1) * 128], hb[:, 0:256].rearrange(
                "p (k t) -> p k t", k=2), ACT.Copy), t, *HT.readers(g))
            banks.give(hb, t)
            tok["h", g] = t

        def stream_b2(g):
            for b in range(NB):
                ns = g * NB + b
                halves = [first_half(ns)] if ns < NG * NB else []
                if ns >= 1 and ns - 1 < NG * NB:
                    halves.append(second_half(ns - 1))
                while halves:
                    for h in list(halves):
                        try:
                            next(h)
                        except StopIteration:
                            halves.remove(h)
                        yield

        qc = [0]

        def stream_c(g):
            t_k1, t_v = tok["ctx", g]
            for m in range(2):
                bk, t = project(wq1, HT[g], m, tok["h", g], t_wq1s)
                t_q = AC.op(lambda e, m=m, bk=bk: e.activation(Q1T[g][:, m, :], bk[:, 0:T], ACT.Identity,
                                                               bias=bq1[:, m:m + 1]), t, t_bq1, *Q1T.readers(g))
                banks.give(bk, t_q)
                yield
            HT.read_by(g, [t])
            units = [(p, j) for p in range(NB // 2) for j in range(4)]
            exp_t, pt_t, av = {}, {}, {}
            N = len(units)
            for i in range(N + LT + LA):
                if i < N:
                    p, j = units[i]
                    n = qc[0] + i
                    ns = g * (NB // 2) + p
                    bk, free = banks.take()
                    r3 = slice(32 * j, 32 * j + 3)
                    r = slice(32 * j, 32 * j + 32)
                    for q in range(4):
                        b, m = 2 * p + q // 2, q % 2
                        tt = slice(b * 128, (b + 1) * 128)
                        t_s = PE.op(lambda e, bk=bk, q=q, m=m, tt=tt, r=r: e.matmul(
                            bk[:, q * 128:(q + 1) * 128], Q1T[g][r, m, tt], K1T[g][r, m, tt],
                            start=(q == 0), stop=False), t_q, t_k1, *free, last=False)
                    t_s = PE.op(lambda e, bk=bk, r3=r3: e.matmul(bk[:, :], onesb[r3, :], maskb[r3, :, :].rearrange(
                        "p a k -> p (a k)"), start=False, stop=True), t_mb, t_ones)
                    late_exp = softmax_part(bk, t_s, PC_, n, stc[ns], 32 ** -0.5,
                                            stc.readers(ns) if j == 0 else [], 4 * j)
                    yield
                if LT <= i < N + LT:
                    n = qc[0] + i - LT
                    bk, free = banks.take()
                    P = PC_[n]
                    t = turns(bk, lambda q, P=P: P[:, q, :], 0, 4, exp_t[i - LT], *free)
                    PC_.read_by(n, [t])
                    t = AC.op(lambda e, bk=bk, n=n: e.activation(PTC[n][:, :, :], bk[:, :].rearrange(
                        "p (i k) -> p i k", i=4), ACT.Copy), t, *PTC.readers(n))
                    banks.give(bk, t)
                    pt_t[i - LT] = t
                    yield
                if i < N:
                    exp_t[i] = late_exp()
                if LT + LA <= i:
                    p, j = units[i - LT - LA]
                    n = qc[0] + i - LT - LA
                    if j == 0:
                        av = {b: banks.take() for b in (2 * p, 2 * p + 1)}
                    for q in range(4):
                        b, m = 2 * p + q // 2, q % 2
                        hd = 4 * m + j
                        o, free = av[b]
                        t = PE.op(lambda e, o=o, n=n, q=q, b=b, hd=hd: e.matmul(
                            o[:, hd * 33:hd * 33 + 33], PTC[n][:, q, :], V1[g][:, b, hd, :], start=True, stop=True),
                            pt_t[i - LT - LA], t_v[b], *free, last=(q == 3))
                    PTC.read_by(n, [t])
                    t_last = t
                    yield
                    if j == 3:
                        for b in (2 * p, 2 * p + 1):
                            ns = g * NB + b
                            o, _ = av[b]
                            st = stc[g * (NB // 2) + p]
                            rc = st[:, 16:24] if b % 2 == 0 else st[:, 24:32]
                            ov = o[:, 0:264].rearrange("p (h d) -> p h d", h=8)
                            xv = oc[ns][:, :].rearrange("p (h d) -> p h d", h=8)
                            t = DV.op(lambda e, rc=rc, ov=ov: e.reciprocal(rc.unsqueeze(2), ov[:, :, 32:33]),
                                      t_last)
                            t = DV.op(lambda e, rc=rc, ov=ov, xv=xv: e.tensor_tensor(
                                xv, ov[:, :, 0:32], rc.unsqueeze(2).to_broadcast([128, 8, 32]), ALU.mult),
                                t, *oc.readers(ns))
                            stc.read_by(g * (NB // 2) + p, [t])
                            banks.give(o, t)
                            yield
                            bt, free = banks.take()
                            t = turns(bt, lambda i, ns=ns: oc[ns][:, i * 128:(i + 1) * 128], 0, 2, t, *free)
                            oc.read_by(ns, [t])
                            t = AC.op(lambda e, bt=bt, ns=ns: e.activation(OT[ns][:, :, :], bt[:, 0:256].rearrange(
                                "p (k t) -> p k t", k=2), ACT.Copy), t, *OT.readers(ns))
                            banks.give(bt, t)
                            yield
                            bo, free = banks.take()
                            t_ot = t
                            for k in range(2):
                                t = PE.op(lambda e, bo=bo, ns=ns, k=k: e.matmul(
                                    bo[:, 0:256], OT[ns][:, k, :], wo[:, k, :], start=(k == 0), stop=(k == 1)),
                                    t_ot, t_wo, *free, last=(k == 1))
                            OT.read_by(ns, [t])
                            yield
                            t = DV.op(lambda e, bo=bo, ns=ns, b=b: e.tensor_tensor(
                                res[ns][:, :], bo[:, 0:256], X2[g][:, b, :], ALU.add), t, *res.readers(ns))
                            t_h = t
                            banks.give(bo, t)
                            t = dma(f"out{ns % 2}", a["out"][g, :, b, :], res[ns][:, :], t)
                            res.read_by(ns, [t])
                            yield
            K1T.read_by(g, [t_s])
            Q1T.read_by(g, [t_s])
            V1.read_by(g, [t_last])
            X2.read_by(g, [t_h])
            qc[0] += N

        lags = ((stream_a1, 0, 8, NG), (stream_a2, 1, 30, NG), (stream_b1, 2, 30, NG), (stream_b2, 3, 30, NG + 1),
                (stream_c, 5, 22, NG))
        for step in range(NG + 5):
            merge([f(step - lag) if 0 <= step - lag < n else None for f, lag, _, n in lags],
                  [w for _, _, w, _ in lags])
        SP.wait([(rec[0], rec[1]) for rec in dma_sems.values()])

        block = ctx.enter_context(nc.Block())
        block.tensor(PE.run)
        block.vector(DV.run)
        block.scalar(AC.run)
        block.gpsimd(GP.run)
        block.sync(SP.run)


def kernel(x, ctx_1024, mask_BxS2_ik0, mask_1xS2_bf0, **w):
    import numpy as np
    import concourse.bacc as bacc
    from concourse.bass_utils import run_bass_kernel_spmd

    w = {k: np.asarray(v) for k, v in w.items()}
    x, c = np.asarray(x), np.asarray(ctx_1024)

    def feature_major(v):
        return np.ascontiguousarray(v.reshape(NG, T, 2, 128).transpose(0, 3, 2, 1))

    def rows(v):
        return np.ascontiguousarray(v.reshape(-1, 128, v.shape[-1]).transpose(1, 0, 2))

    def cols(v):
        return v.reshape(-1, 128).T

    p = np.arange(128)
    pcols = np.zeros((128, 20), np.float32)
    for at, n, name in ((0, 2, "L0_xattn_bq"), (2, 2, "L0_xattn_bk"), (4, 2, "L1_xattn_m_norm_w"),
                        (6, 4, "L1_xattn_gnorm_w"), (10, 2, "L1_xattn_ca_ln_w"), (12, 2, "L1_xattn_ca_ln_b")):
        pcols[:, at:at + n] = cols(w[name])
    arrays = {
        "ident": np.eye(128, dtype=np.float32),
        "par": np.stack([(p // 16 + 1) % 2, (p // 16) % 2], 1).astype(np.float32),
        "sel": np.stack([p % 32 == i for i in range(3)], 1).astype(np.float32),
        "pcols": pcols,
        "convp": np.ascontiguousarray(np.concatenate(
            [w["L1_xattn_conv_w"].reshape(6, 128, 4), w["L1_xattn_conv_b"].reshape(6, 128, 1)], 2).transpose(1, 0, 2)),
        "heads": np.concatenate([w["L1_xattn_dt_bias"], w["L1_xattn_A_log"], w["L1_xattn_D_skip"]])[None],
        "maskT": np.ascontiguousarray(np.asarray(mask_BxS2_ik0).T),
        "pad": np.asarray(mask_1xS2_bf0),
        "xT": feature_major(x), "cT": feature_major(c),
        "xt": np.ascontiguousarray(x.reshape(NG, NB, S, D).transpose(0, 2, 1, 3)),
        "wq": rows(w["L0_xattn_Wq"]), "wk": rows(w["L0_xattn_Wk"]),
        "wv": rows(np.concatenate([w["L0_xattn_Wv"], w["L1_xattn_Wv"]], 1)),
        "wk1": rows(w["L1_xattn_Wk"]), "wq1": rows(w["L1_xattn_Wq"]), "wo": rows(w["L1_xattn_Wo"]),
        "win": rows(w["L1_xattn_in_proj_w"]), "wout": rows(w["L1_xattn_out_proj_w"]),
        "bv": w["L0_xattn_bv"], "gamma": w["L0_xattn_gamma"], "beta": w["L0_xattn_beta"],
    }
    nc = bacc.Bacc("TRN2", target_bir_lowering=False, num_devices=1)
    args, ins = {}, {}
    for name, v in arrays.items():
        ins["in_" + name] = v
        args[name] = nc.dram_tensor("in_" + name, v.shape, mybir.dt.from_np(v.dtype), kind="ExternalInput").ap()
    args["out"] = nc.dram_tensor("out_x", (NG, S, NB, D), F32, kind="ExternalOutput").ap()
    program(nc, args)
    r = run_bass_kernel_spmd(nc, [ins], core_ids=[0])
    out = r.results[0]["out_x"]
    return np.ascontiguousarray(out.transpose(0, 2, 1, 3)).reshape(NG * NB, S, D)
```

```python
from contextlib import ExitStack

import concourse.bass as bass
from concourse import mybir

F32 = mybir.dt.float32
BF16 = mybir.dt.bfloat16
ALU = mybir.AluOpType
ACT = mybir.ActivationFunctionType
AX_X = mybir.AxisListType.X

NG = 32
NB = 2
S = 128
D = 256
T = NB * S
EPS = 1e-5
LT = 3
LTC = 4
LA = 2
BIG = 3.0e38
NPROJ = 1288
SHARE = (8, 34, 30, 31.0, 22)
PHASE = (-1.5, 0.5, 0.2, 2.8, 0.5)


class Engine:

    def __init__(self, sem):
        self.sem, self.n, self.q, self.met = sem, 0, [], {}

    def wait(self, tokens):
        for sem, value in tokens:
            if self.met.get(id(sem), 0) < value:
                self.met[id(sem)] = value
                self.q.append(lambda e, s=sem, v=value: e.wait_ge(s, v))

    def op(self, fn, *tokens, last=True):
        self.wait(tokens)
        if not last:
            self.q.append(fn)
            return None
        self.n += 1
        self.q.append(lambda e: fn(e).then_inc(self.sem, 1))
        return (self.sem, self.n)

    def run(self, e):
        for f in self.q:
            f(e)


class Banks:

    def __init__(self, tiles):
        self.idle = [(t, None) for t in tiles]

    def take(self):
        tile, token = self.idle.pop(0)
        return tile, ([token] if token else [])

    def give(self, tile, token):
        self.idle.append((tile, token))


class Slots:

    def __init__(self, tiles):
        self.tiles, self.free = tiles, [[] for _ in tiles]

    def __getitem__(self, i):
        return self.tiles[i % len(self.tiles)]

    def readers(self, i):
        return self.free[i % len(self.tiles)]

    def read_by(self, i, tokens):
        self.free[i % len(self.tiles)] = list(tokens)


def merge(streams, weights, phases):
    done = [0] * len(streams)
    live = [s is not None for s in streams]
    while any(live):
        i = min((k for k in range(len(streams)) if live[k]), key=lambda k: (done[k] + phases[k]) / weights[k])
        try:
            next(streams[i])
            done[i] += 1
        except StopIteration:
            live[i] = False
    return done


def program(nc, a):
    with ExitStack() as ctx:
        def sb(name, shape, dt=F32):
            return ctx.enter_context(nc.sbuf_tensor(name, shape, dt))

        def sem(name):
            return ctx.enter_context(nc.semaphore(name))

        def slots(name, n, shape, dt=F32):
            return Slots([sb(f"{name}{i}", shape, dt) for i in range(n)])

        PE, DV, AC, GP, SP = (Engine(sem(f"s_{n}")) for n in ("pe", "dve", "act", "pool", "sp"))
        banks = Banks([ctx.enter_context(nc.psum_tensor(f"bank{i}", [128, 512], F32)) for i in range(8)])
        dma_sems = {}

        def dma(name, out, in_, *tokens):
            if name not in dma_sems:
                dma_sems[name] = [sem("d_" + name), 0]
            rec = dma_sems[name]
            SP.wait(tokens)
            if rec[1]:
                SP.wait([(rec[0], rec[1])])
            rec[1] += 16
            SP.q.append(lambda e, s=rec[0]: e.dma_start(out, in_).then_inc(s, 16))
            return (rec[0], rec[1])

        ident = sb("ident", [128, 128])
        id8 = sb("id8", [128, 8, 128])
        par = sb("par", [128, 2])
        sel = sb("sel", [128, 3])
        onesb = sb("onesb", [128, 128], BF16)
        wq = sb("wq", [128, 2, 256])
        wk = sb("wk", [128, 2, 256])
        wv = sb("wv", [128, 2, 512])
        wk1 = sb("wk1", [128, 2, 256])
        wq1 = sb("wq1", [128, 2, 256])
        wo = sb("wo", [128, 2, 256])
        win = sb("win", [128, 2, NPROJ])
        wout = sb("wout", [128, 4, 256])
        pc = sb("pc", [128, 20])
        cw = sb("cw", [128, 6, 5])
        gam = sb("gam", [128, 256])
        bet = sb("bet", [128, 256])
        h8 = sb("h8", [128, 2, 8])
        negA = sb("negA", [128, 8])
        mrow = sb("mrow", [128, 128], mybir.dt.uint8)
        mi = sb("mi", [128, 64], mybir.dt.int32)
        sq = sb("sq", [128, 64])
        keep = sb("keep", [128, 128])
        negm = sb("negm", [128, 128])
        maskb = sb("maskb", [128, 4, 128], BF16)
        bvr = sb("bvr", [128, 256])
        vbias = sb("vbias", [128, 512], BF16)
        mhalf = sb("mhalf", [128, 1])
        ones1 = sb("ones1", [128, 1])
        kb = sb("kb", [128, 2, 2])
        bq1 = sb("bq1", [128, 2])

        xT = slots("xT", 1, [128, 2, T])
        cT = slots("cT", 1, [128, 2, T])
        xt = slots("xt", 2, [128, NB, D])
        OA = slots("OA", 1, [128, 512])
        QT = slots("QT", 2, [128, 2, T])
        KT = slots("KT", 2, [128, 2, NB, 2, 128])
        V0 = slots("V0", 2, [128, NB, 16, 32])
        K1T = slots("K1T", 6, [128, 2, T])
        V1 = slots("V1", 6, [128, NB, 8, 32])
        PA = slots("PA", LT + 1, [128, 4, 128])
        PTA = slots("PTA", LA + 1, [128, 4, 128])
        PC_ = slots("PC", LTC + 1, [128, 4, 128])
        PTC = slots("PTC", LA + 2, [128, 4, 128])
        X2 = slots("X2", 5, [128, NB, D])
        sta = slots("sta", 4, [128, 48])
        stb = slots("stb", 4, [128, 16])
        stn = slots("stn", 4, [128, 1])
        stc = slots("stc", 4, [128, 32])
        xa = slots("xa", 2, [128, 256])
        xn = slots("xn", 2, [128, 256])
        xnT = slots("xnT", 2, [128, 2, T])
        XP = slots("XP", 3, [128, NB, 131])
        ACC = slots("ACC", 3, [128, NB, 128])
        XC = slots("XC", 2, [128, 6, T])
        SZ = slots("SZ", 2, [128, 512])
        dts = sb("dts", [128, 8, 8 * NB])
        dtt = slots("dtt", 3, [128, 8 * NB])
        decT = slots("decT", 2, [8 * NB, 128])
        DB = slots("DB", 2, [128, 1024])
        L = slots("L", 1, [128, 8, 128])
        XH = slots("XH", 1, [128, 512])
        DX = slots("DX", 2, [128, 512])
        Y = slots("Y", 2, [128, 512])
        SQ = slots("SQ", 1, [128, 4, 128])
        xh = slots("xh", 2, [128, 256])
        HT = slots("HT", 2, [128, 2, T])
        Q1T = slots("Q1T", 2, [128, 2, T])
        OT = slots("OT", 1, [128, 4, 128])
        res = slots("res", 1, [128, NB, 256])
        junk = sb("junk", [128, 256], BF16)
        scratch = nc.dram_tensor("dec_scratch", [NG, NB * 8 * 128], F32, kind="Internal").ap()

        s0, s1, s2 = SQ[0][:, 0:2, :], SQ[0][:, 2, :].bitcast(BF16), Y[0][:, 0:256]
        s0 = s0.rearrange("p a b -> p (a b)")

        def bcast(v, n):
            return v.rearrange("(a n) -> a n", a=1).to_broadcast([128, n])

        consts = dma("c_id", ident[:, :], a["ident"])
        t_sel = dma("c_sel", sel[:, :], a["sel"])
        t_par = dma("c_par", par[:, :], a["par"])
        t_pc = dma("c_pc", pc[:, :], a["pcols"])
        t_cw = dma("c_cw", cw[:, :, :], a["convp"])
        t_mi = dma("c_mi", mi[:, :], a["maskT"])
        t_w = [dma("w_" + n, t[:, :, :], a[n]) for n, t in
               (("wq", wq), ("wk", wk), ("wv", wv), ("wk1", wk1))]

        loads = {}

        def load(name, ring, g):
            if g < NG:
                loads[name, g] = dma(f"{name}{g % len(ring.tiles)}", ring[g][:, :, :], a[name][g], *ring.readers(g))

        load("xT", xT, 0)
        load("cT", cT, 0)
        load("xt", xt, 0)
        t_h8 = dma("c_h8", h8[:, :, :], a["heads"].rearrange("a (b c) -> a b c", b=2).to_broadcast([128, 2, 8]))
        t_bv = dma("c_bv", bvr[:, :], bcast(a["bv"], 256))
        t_mr = dma("c_mr", mrow[:, :], a["pad"].to_broadcast([128, 128]))
        t_gam = dma("c_gam", gam[:, :], bcast(a["gamma"], 256))
        t_bet = dma("c_bet", bet[:, :], bcast(a["beta"], 256))
        t_win = dma("w_win", win[:, :, :], a["win"])
        t_wout = dma("w_wout", wout[:, :, :], a["wout"])
        t_wq1 = dma("w_wq1", wq1[:, :, :], a["wq1"])
        t_wo = dma("w_wo", wo[:, :, :], a["wo"])

        t_ones = GP.op(lambda e: e.memset(onesb[:, :], 1.0))
        t_mh = GP.op(lambda e: e.memset(mhalf[:, :], -0.5))
        t_one = GP.op(lambda e: e.memset(ones1[:, :], 1.0))
        t_pad = []
        for i in range(3):
            t_pad.append(GP.op(lambda e, i=i: e.memset(XP[i][:, :, 0:3], 0.0)))
        for i in range(2):
            t_pad.append(GP.op(lambda e, i=i: e.memset(decT[i][:, 0:1], 0.0)))
            t = GP.op(lambda e, i=i: e.memset(V0[i][:, :, :, 16:32], 0.0))
            t_pad.append(GP.op(lambda e, i=i: e.memset(V0[i][:, :, :, 16:17], 1.0), t))
        t_id8 = [GP.op(lambda e, h=h: e.tensor_copy(id8[:, h, :], ident[:, :]), consts) for h in range(8)][-1]
        t_sq = DV.op(lambda e: e.tensor_scalar(sq[:, :], mi[:, :], 0.0, 0.25, ALU.not_equal, ALU.mult), t_mi)
        t_kb = DV.op(lambda e: e.tensor_scalar(kb[:, 0, :], pc[:, 2:4], par[:, 0:1], None, ALU.mult), t_pc, t_par)
        t_k1 = DV.op(lambda e: e.tensor_scalar(s0[:, 0:1], par[:, 0:1], -BIG, None, ALU.mult), t_par)
        t_kb1 = DV.op(lambda e: e.tensor_scalar(kb[:, 1, :], pc[:, 2:4], s0[:, 0:1], None, ALU.add), t_k1)
        t_keep = DV.op(lambda e: e.tensor_scalar(keep[:, :], mrow[:, :], 0.0, None, ALU.is_equal), t_mr)
        t_neg = DV.op(lambda e: e.tensor_scalar(negm[:, :], mrow[:, :], 0.0, -1.0e9 * 32 ** 0.5,
                                                ALU.not_equal, ALU.mult), t_mr)

        def split3(src, n, dst, token):
            t = DV.op(lambda e: e.tensor_copy(s1[:, 0:n], src), token, t_sel)
            p = DV.op(lambda e: e.tensor_scalar(s0[:, 0:n], s1[:, 0:n], sel[:, 0:1], None, ALU.mult), t)
            r = DV.op(lambda e: e.tensor_tensor(s2[:, 0:n], src, s1[:, 0:n], ALU.subtract), t)
            for i in (1, 2):
                t = DV.op(lambda e: e.tensor_copy(s1[:, 0:n], s2[:, 0:n]), r, p)
                p = DV.op(lambda e, i=i: e.scalar_tensor_tensor(out=s0[:, 0:n], in0=s1[:, 0:n], scalar=sel[:, i:i + 1],
                                                                in1=s0[:, 0:n], op0=ALU.mult, op1=ALU.add), t, p)
                r = DV.op(lambda e: e.tensor_tensor(s2[:, 0:n], s2[:, 0:n], s1[:, 0:n], ALU.subtract), t)
            return DV.op(lambda e: e.tensor_copy(dst, s0[:, 0:n]), p, r)

        t_vb0 = DV.op(lambda e: e.memset(vbias[:, 256:512], 0.0))
        t_vb = split3(bvr[:, :], 256, vbias[:, 0:256], t_bv)
        t_mb = split3(negm[:, :], 128, maskb[:, 0, :], t_neg)
        for i in range(1, 4):
            t_mb = DV.op(lambda e, i=i: e.tensor_copy(maskb[:, i, :], maskb[:, 0, :]), t_mb)
        for k in range(2):
            ins = ((0, 512, 0.5), (512, NPROJ, 1.0))
            for lo, hi, c in ins:
                t_wz = GP.op(lambda e, k=k, lo=lo, hi=hi, c=c: e.tensor_scalar(
                    win[:, k, lo:hi], win[:, k, lo:hi], pc[:, 4 + k:5 + k], c, ALU.mult, ALU.mult), t_win, t_pc)
        for k in range(4):
            t_wo2 = GP.op(lambda e, k=k: e.tensor_scalar(
                wout[:, k, :], wout[:, k, :], pc[:, 6 + k:7 + k], None, ALU.mult), t_wout, t_pc)
        t_cw2 = GP.op(lambda e: e.tensor_scalar(cw[:, :, :], cw[:, :, :], 0.5, None, ALU.mult), t_cw)
        bk, w = banks.take()
        for m in range(2):
            for k in range(2):
                t_b1 = PE.op(lambda e, m=m, k=k: e.matmul(bk[:, m:m + 1], wq1[:, k, m * 128:(m + 1) * 128],
                                                          pc[:, 12 + k:13 + k], start=(k == 0), stop=(k == 1)),
                             t_wq1, t_pc, *w)
        t_bq1 = DV.op(lambda e: e.tensor_copy(bq1[:, :], bk[:, 0:2]), t_b1)
        banks.give(bk, t_bq1)
        for k in range(2):
            t_wq1s = GP.op(lambda e, k=k: e.tensor_scalar(wq1[:, k, :], wq1[:, k, :], pc[:, 10 + k:11 + k], None,
                                                          ALU.mult), t_b1)
        t_ea = AC.op(lambda e: e.activation(negA[:, :], h8[:, 1, :], ACT.Exp), t_h8)
        t_nA = DV.op(lambda e: e.tensor_scalar(negA[:, :], negA[:, :], -1.0, None, ALU.mult), t_ea)

        tok = {}

        def project(w_ap, src, m, *tokens):
            bk, free = banks.take()
            for k in range(2):
                t = PE.op(lambda e, k=k: e.matmul(bk[:, 0:T], w_ap[:, k, m * 128:(m + 1) * 128], src[:, k, :],
                                                  start=(k == 0), stop=(k == 1)), *tokens, *free, last=(k == 1))
            return bk, t

        def turns(bk, src, col, n, *tokens, last=True):
            for i in range(n):
                t = PE.op(lambda e, i=i: e.transpose(bk[:, col + i * 128:col + (i + 1) * 128], src(i), ident[:, :]),
                          *tokens, consts, last=(last and i == n - 1))
            return t

        def softmax_part(bk, t_s, ring, n, st, scale, tokens, mcol):
            P = ring[n]
            v = bk[:, :].rearrange("p (i k) -> p i k", i=4)
            mx = st[:, mcol:mcol + 4]
            t_m = DV.op(lambda e: e.tensor_reduce(mx, v, AX_X, ALU.max), t_s, *tokens)
            t_d = DV.op(lambda e: e.tensor_tensor(P[:, :, :], v, mx.unsqueeze(2).to_broadcast([128, 4, 128]),
                                                  ALU.subtract), t_m, *ring.readers(n))
            banks.give(bk, t_d)
            return lambda: AC.op(lambda e: e.activation(P[:, :, :], P[:, :, :], ACT.Exp, scale=scale), t_d)

        def layer_stats(src, st, c, token, *more):
            t = DV.op(lambda e: e.bn_stats(st[:, c + 2:c + 8], src), token, *more)
            t = DV.op(lambda e: e.bn_aggr(st[:, c:c + 2], st[:, c + 2:c + 8]), t)
            t = GP.op(lambda e: e.tensor_scalar(st[:, c + 1:c + 2], st[:, c + 1:c + 2], EPS, None, ALU.add), t)
            return GP.op(lambda e: e.tensor_tensor(st[:, c + 1:c + 2], st[:, c + 1:c + 2], mhalf[:, :], ALU.pow), t, t_mh)

        qa = [0]

        def stream_a1(g):
            t_x, t_c = (loads[n, g] for n in ("xT", "cT"))
            readers_q, readers_k = [], []
            for m in range(2):
                bk, t = project(wq, xT[g], m, t_x, t_w[0])
                t_q = AC.op(lambda e, m=m, bk=bk: e.activation(QT[g][:, m, :], bk[:, 0:T], ACT.Relu, bias=pc[:, m:m + 1]),
                            t, t_pc, *QT.readers(g))
                banks.give(bk, t_q)
                yield
            xT.read_by(g, [t])
            load("xT", xT, g + 1)
            for m in range(2):
                bk, t = project(wk, cT[g], m, t_c, t_w[1])
                v = bk[:, 0:T].rearrange("p (b k) -> p b k", b=NB)
                t_k = AC.op(lambda e, m=m, v=v: e.activation(KT[g][:, m, :, 0, :], v, ACT.Relu, bias=kb[:, 0, m:m + 1],
                                                             scale=par[:, 0:1]), t, t_kb, t_par, *KT.readers(g))
                t_k2 = DV.op(lambda e, m=m, v=v: e.tensor_scalar(KT[g][:, m, :, 1, :], v, kb[:, 1, m:m + 1], 0.0,
                                                                 ALU.add, ALU.max), t_k, t_kb1, *KT.readers(g))
                banks.give(bk, t_k2)
                yield
            for m in range(2):
                bk, t = project(wk1, cT[g], m, t_c, t_w[3])
                v = bk[:, 0:T].rearrange("p (b k) -> p b k", b=NB)
                t_k1 = DV.op(lambda e, m=m, v=v: e.tensor_tensor(
                    K1T[g][:, m, :].rearrange("p (b k) -> p b k", b=NB), v,
                    keep[:, :].unsqueeze(1).to_broadcast([128, NB, 128]), ALU.mult), t, t_keep, *K1T.readers(g))
                banks.give(bk, t_k1)
                yield
            t_v = []
            for b in range(NB):
                bk, free = banks.take()
                PE.op(lambda e, bk=bk: e.matmul(bk[:, :], onesb[0:3, :], vbias[0:3, :], start=True, stop=False),
                      t_ones, t_vb, t_vb0, *free, last=False)
                for k in range(2):
                    t = PE.op(lambda e, bk=bk, k=k, b=b: e.matmul(bk[:, :], cT[g][:, k, b * 128:(b + 1) * 128],
                                                                  wv[:, k, :], start=False, stop=(k == 1)), t_w[2],
                              last=(k == 1))
                AC.op(lambda e, bk=bk, b=b: e.activation(
                    V0[g][:, b, :, 0:16], bk[:, 0:256].rearrange("p (h d) -> p h d", h=16), ACT.Relu),
                    t, *t_pad, *V0.readers(g))
                t_v.append(AC.op(lambda e, bk=bk, b=b: e.activation(
                    V1[g][:, b, :, :], bk[:, 256:512].rearrange("p (h d) -> p h d", h=8), ACT.Copy),
                    t, *V1.readers(g)))
                banks.give(bk, t_v[-1])
                yield
            cT.read_by(g, [t])
            load("cT", cT, g + 1)
            tok["ctx", g] = (t_k1, t_v)
            tok["qkv", g] = (t_q, t_k, t_k2, t_v)

        def stream_a2(g):
            t_q, t_k, t_k2, t_v = tok["qkv", g]
            t_xt = loads["xt", g]
            load("xt", xt, g + 1)

            units = [(b, j) for b in range(NB) for j in range(4)]
            exp_t, pt_t, av = {}, {}, {}
            N = len(units)
            t_last = None
            for i in range(N + LT + LA):
                if i < N:
                    b, j = units[i]
                    n = qa[0] + i
                    bk, free = banks.take()
                    r = slice(32 * j, 32 * j + 32)
                    for m in range(2):
                        t_s = PE.op(lambda e, bk=bk, m=m, b=b, r=r: e.matmul(
                            bk[:, m * 256:(m + 1) * 256], QT[g][r, m, b * 128:(b + 1) * 128], KT[g][r, m, b, :, :],
                            start=True, stop=True), t_q, t_k, t_k2, *free, last=(m == 1))
                    ns = g * NB + b
                    late_exp = softmax_part(bk, t_s, PA, n, sta[ns], sq[:, ns:ns + 1],
                                            [t_sq, *(sta.readers(ns) if j == 0 else [])], 4 * j)
                    yield
                if LT <= i < N + LT:
                    b, j = units[i - LT]
                    n = qa[0] + i - LT
                    bk, free = banks.take()
                    P = PA[n]
                    t = turns(bk, lambda q, P=P: P[:, q, :], 0, 4, exp_t[i - LT], *free)
                    PA.read_by(n, [t])
                    t = AC.op(lambda e, bk=bk, n=n: e.activation(PTA[n][:, :, :], bk[:, :].rearrange(
                        "p (i k) -> p i k", i=4), ACT.Copy), t, *PTA.readers(n))
                    banks.give(bk, t)
                    pt_t[i - LT] = t
                    yield
                if i < N:
                    exp_t[i] = late_exp()
                if LT + LA <= i:
                    b, j = units[i - LT - LA]
                    n = qa[0] + i - LT - LA
                    if j == 0:
                        av[b] = banks.take()
                    o, free = av[b]
                    for q in range(4):
                        t = PE.op(lambda e, o=o, n=n, q=q, b=b, j=j: e.matmul(
                            o[32 * q:32 * q + 32, j * 128:(j + 1) * 128], V0[g][:, b, 4 * j + q, :],
                            PTA[n][:, q, :], start=True, stop=True),
                            pt_t[i - LT - LA], t_v[b], *free, last=(q == 3))
                    PTA.read_by(n, [t])
                    t_last = t
                    if j == 3:
                        yield
                        ns = g * NB + b
                        t = AC.op(lambda e, o=o, ns=ns: e.activation(OA[ns][:, :], o[:, :], ACT.Copy), t, *OA.readers(ns))
                        banks.give(o, t)
                        yield
                        o, free = banks.take()
                        t = turns(o, lambda i, ns=ns: OA[ns][:, i * 128:(i + 1) * 128], 0, 4, t, *free)
                        OA.read_by(ns, [t])
                        yield
                        st = sta[ns]
                        ov = o[:, :].rearrange("p (h d) -> p h d", h=16)
                        xv = xa[ns][:, :].rearrange("p (h d) -> p h d", h=16)
                        t = DV.op(lambda e, st=st, ov=ov: e.reciprocal(st[:, 16:32].unsqueeze(2), ov[:, :, 16:17]), t)
                        t = DV.op(lambda e, st=st, ov=ov, xv=xv: e.tensor_tensor(
                            xv, ov[:, :, 0:16], st[:, 16:32].unsqueeze(2).to_broadcast([128, 16, 16]), ALU.mult),
                            t, *xa.readers(ns))
                        banks.give(o, t)
                        t = GP.op(lambda e, ns=ns, b=b: e.tensor_tensor(xa[ns][:, :], xa[ns][:, :], xt[g][:, b, :],
                                                                        ALU.add), t, t_xt)
                        t_xr = t
                        yield
                        t = layer_stats(xa[ns][:, :], st, 32, t)
                        x2 = X2[g][:, b, :]
                        t = DV.op(lambda e, ns=ns, st=st: e.tensor_scalar(
                            xa[ns][:, :], xa[ns][:, :], st[:, 32:33], st[:, 33:34], ALU.subtract, ALU.mult), t)
                        sta.read_by(ns, [t])
                        yield
                        t = GP.op(lambda e, ns=ns, x2=x2: e.tensor_tensor(x2, xa[ns][:, :], gam[:, :], ALU.mult),
                                  t, t_gam, *X2.readers(g))
                        xa.read_by(ns, [t])
                        t = GP.op(lambda e, x2=x2: e.tensor_tensor(x2, x2, bet[:, :], ALU.add), t, t_bet)
                        tok["x2", g, b] = t
                    yield
            QT.read_by(g, [t_s])
            KT.read_by(g, [t_s])
            V0.read_by(g, [t_last])
            xt.read_by(g, [t_xr])
            qa[0] += N

        def stream_b1(g):
            t_r = []
            for b in range(NB):
                ns = g * NB + b
                x2 = X2[g][:, b, :]
                t = AC.op(lambda e, x2=x2, ns=ns: e.activation(junk[:, 0:256], x2, ACT.Square, scale=1.0 / 16,
                                                               accum_out=stn[ns][:, 0:1]),
                          tok["x2", g, b], (AC.sem, AC.n), *stn.readers(ns))
                t = GP.op(lambda e, ns=ns: e.tensor_scalar(stn[ns][:, :], stn[ns][:, :], EPS, None, ALU.add), t)
                t_r.append(GP.op(lambda e, ns=ns: e.tensor_tensor(stn[ns][:, :], stn[ns][:, :], mhalf[:, :], ALU.pow),
                                 t, t_mh))
                yield
            t_n = []
            for b in range(NB):
                ns = g * NB + b
                t = DV.op(lambda e, ns=ns, b=b: e.tensor_scalar(xn[ns][:, :], X2[g][:, b, :], stn[ns][:, 0:1], None,
                                                                ALU.mult), t_r[b], *xn.readers(ns))
                stn.read_by(ns, [t])
                t_n.append(t)
            yield
            yield
            bk, free = banks.take()
            for b in range(NB):
                ns = g * NB + b
                t = turns(bk, lambda i, ns=ns: xn[ns][:, i * 128:(i + 1) * 128], b * 256, 2, t_n[b], *free)
                xn.read_by(ns, [t])
            v = bk[:, :].rearrange("p (b k t) -> p k b t", b=NB, k=2)
            o = xnT[g][:, :, :].rearrange("p k (b t) -> p k b t", b=NB)
            for k in range(2):
                t = AC.op(lambda e, v=v, o=o, k=k: e.activation(o[:, k], v[:, k], ACT.Copy), t, *xnT.readers(g))
            banks.give(bk, t)
            t_n = t
            tok["xnT", g] = t
            yield
            yield

            d = [dts[:, i, :] for i in range(8)]
            dt = dtt[g][:, :]
            v4 = lambda x: x.rearrange("p (b h) -> p b h", b=NB)
            bc = lambda x: x.unsqueeze(1).to_broadcast([128, NB, 8])

            def steps():
                bk, free = banks.take()
                for b in range(NB):
                    for k in range(2):
                        t = PE.op(lambda e, bk=bk, k=k, b=b: e.matmul(
                            bk[:, b * 8:b * 8 + 8], xnT[g][:, k, b * 128:(b + 1) * 128], win[:, k, 1280:1288],
                            start=(k == 0), stop=(k == 1)), t_n, t_wz, *free, last=(b == NB - 1 and k == 1))
                t = DV.op(lambda e: e.tensor_tensor(v4(d[0]), v4(bk[:, 0:8 * NB]), bc(h8[:, 0, :]), ALU.add), t, t_h8,
                          *tok.get("dts", []))
                banks.give(bk, t)
                yield
                t = AC.op(lambda e: e.activation(d[1], d[0], ACT.Abs), t)
                t_e = AC.op(lambda e: e.activation(d[1], d[1], ACT.Exp, scale=-1.0), t)
                yield
                t_w = DV.op(lambda e: e.tensor_scalar(d[2], d[1], 1.0, None, ALU.add), t_e)
                t_w1 = DV.op(lambda e: e.tensor_scalar(d[4], d[2], 1.0, None, ALU.subtract), t_w)
                yield
                t_l = AC.op(lambda e: e.activation(d[3], d[2], ACT.Ln), t_w)
                t = GP.op(lambda e: e.tensor_scalar(d[5], d[4], 0.0, None, ALU.is_equal), t_w1)
                t_g = GP.op(lambda e: e.tensor_tensor(d[5], d[5], d[1], ALU.mult), t)
                yield
                t = DV.op(lambda e: e.tensor_scalar(d[4], d[4], 1e-30, None, ALU.max), t_g)
                t = DV.op(lambda e: e.reciprocal(d[6], d[4]), t)
                t = DV.op(lambda e: e.tensor_tensor(d[6], d[6], d[1], ALU.mult), t)
                t = DV.op(lambda e: e.tensor_tensor(d[6], d[6], d[3], ALU.mult), t, t_l)
                t = DV.op(lambda e: e.tensor_tensor(d[6], d[6], d[5], ALU.add), t)
                t_dt = DV.op(lambda e: e.scalar_tensor_tensor(out=dt, in0=d[0], scalar=0.0, in1=d[6], op0=ALU.max,
                                                              op1=ALU.add), t, *dtt.readers(g))
                tok["dt", g] = t_dt
                t = DV.op(lambda e: e.tensor_tensor(v4(d[7]), v4(dt), bc(negA[:, :]), ALU.mult), t_dt, t_nA)
                yield
                t_a = AC.op(lambda e: e.activation(d[7], d[7], ACT.Exp), t)
                yield
                yield
                bd, free = banks.take()
                t = PE.op(lambda e: e.transpose(bd[0:8 * NB, 0:128], d[7], ident[:, :]), t_a, *free)
                tok["dts"] = [t, t_dt]
                t = DV.op(lambda e: e.tensor_copy(decT[g][:, 1:128], bd[0:8 * NB, 1:128]), t, *decT.readers(g),
                          *t_pad)
                banks.give(bd, t)
                t = dma(f"scr{g % 2}", scratch[g].rearrange("(p t) -> p t", p=8 * NB), decT[g][:, :], t)
                decT.read_by(g, [t])
                tok["scr", g] = t

            ds = steps()
            acc_t = {}
            for i in range(8):
                next(ds, None)
                if i < 6:
                    n, c = g * 6 + i, i
                    bk, t = project(win[:, :, 512:1280], xnT[g], c, t_n, t_wz)
                    v = bk[:, 0:T].rearrange("p (b t) -> p b t", b=NB)
                    t1 = AC.op(lambda e, v=v, n=n: e.activation(XP[n][:, :, 3:131], v, ACT.Copy), t, *t_pad,
                               *XP.readers(n))
                    t2 = AC.op(lambda e, v=v, n=n, c=c: e.activation(
                        ACC[n][:, :, :], v, ACT.Identity, bias=cw[:, c, 4:5], scale=cw[:, c, 3:4]),
                        t, t_cw2, *ACC.readers(n))
                    banks.give(bk, t2)
                    acc_t[i] = t1, t2
                    yield
                if 1 <= i < 7:
                    n, c = g * 6 + i - 1, i - 1
                    t1, t = acc_t[i - 1]
                    for k in range(3):
                        t = DV.op(lambda e, k=k, n=n, c=c: e.scalar_tensor_tensor(
                            out=ACC[n][:, :, :], in0=XP[n][:, :, k:k + 128], scalar=cw[:, c, k:k + 1],
                            in1=ACC[n][:, :, :], op0=ALU.mult, op1=ALU.add), t, t1, t_cw2)
                    XP.read_by(n, [t])
                    acc_t[i - 1] = t
                    yield
                if i >= 2:
                    n, c = g * 6 + i - 2, i - 2
                    xc = XC[g][:, c, :].rearrange("p (b t) -> p b t", b=NB)
                    t = AC.op(lambda e, n=n, xc=xc: e.activation(xc, ACC[n][:, :, :], ACT.Tanh), acc_t[i - 2],
                              *XC.readers(g))
                    yield
                    t_xc = DV.op(lambda e, n=n, xc=xc: e.scalar_tensor_tensor(
                        out=xc, in0=xc, scalar=1.0, in1=ACC[n][:, :, :], op0=ALU.add, op1=ALU.mult), t)
                    ACC.read_by(n, [t_xc])
                    yield
            for _ in ds:
                yield
            tok["xc", g] = t_xc

        t_db = {}

        def fetch(ns):
            g, b = ns // NB, ns % NB
            t_db[ns] = dma(f"db{ns % 2}", DB[ns][:, :], scratch[g, b * 1024:(b + 1) * 1024].rearrange(
                "(a n) -> a n", a=1).to_broadcast([128, 1024]), tok["scr", g], *DB.readers(ns))

        cv = lambda x: x.rearrange("p (c t) -> p c t", c=4)
        hv = lambda x: x.rearrange("p (h d) -> p h d", h=8)

        def first_half(ns):
            g, b = ns // NB, ns % NB
            t_xc, t_dt = tok["xc", g], tok["dt", g]
            ts = slice(b * 128, (b + 1) * 128)
            if ns not in t_db:
                fetch(ns)
            bx, free = banks.take()
            t_x = turns(bx, lambda i: XC[g][:, i, ts], 0, 4, t_xc, *free)
            t = AC.op(lambda e: e.activation(XH[ns][:, :], bx[:, :], ACT.Copy), t_x, *XH.readers(ns))
            banks.give(bx, t)
            t_dx = GP.op(lambda e: e.tensor_tensor(
                cv(DX[ns][:, :]), XC[g][:, 0:4, ts],
                pc[:, 14:18].unsqueeze(2).to_broadcast([128, 4, 128]), ALU.mult), t_xc, t_pc, *DX.readers(ns))
            t_xd = GP.op(lambda e: e.tensor_tensor(
                hv(XH[ns][:, :]), hv(XH[ns][:, :]),
                dtt[g][:, b * 8:b * 8 + 8].unsqueeze(2).to_broadcast([128, 8, 64]), ALU.mult), t, t_dt)
            t_l = DV.op(lambda e: e.tensor_tensor_scan(
                L[ns][:, :, :].rearrange("p h t -> p (h t)"), DB[ns][:, :],
                id8[:, :, :].rearrange("p h t -> p (h t)"), 0.0, ALU.mult, ALU.add),
                t_db[ns], t_id8, *L.readers(ns))
            DB.read_by(ns, [t_l])
            yield
            bg, free = banks.take()
            t_gm = PE.op(lambda e: e.matmul(bg[:, 0:128], XC[g][:, 4, ts], XC[g][:, 5, ts],
                                            start=True, stop=True), t_xc, *free)
            yield
            t_m = DV.op(lambda e: e.tensor_tensor(
                L[ns][:, :, :], L[ns][:, :, :], bg[:, 0:128].unsqueeze(1).to_broadcast([128, 8, 128]), ALU.mult),
                t_l, t_gm)
            banks.give(bg, t_m)
            if b == NB - 1:
                XC.read_by(g, [t_gm, t_dx])
            yield
            bz, free = banks.take()
            for c in range(4):
                for k in range(2):
                    t_x = PE.op(lambda e, c=c, k=k: e.matmul(
                        bz[:, c * 128:(c + 1) * 128], win[:, k, c * 128:(c + 1) * 128], xnT[g][:, k, ts],
                        start=(k == 0), stop=(k == 1)), tok["xnT", g], *free, last=(c == 3 and k == 1))
            if b == NB - 1:
                xnT.read_by(g, [t_x])
            t = AC.op(lambda e: e.activation(SZ[ns][:, :], bz[:, :], ACT.Tanh), t_x, *SZ.readers(ns))
            yield
            t_sz = DV.op(lambda e: e.scalar_tensor_tensor(
                out=SZ[ns][:, :], in0=SZ[ns][:, :], scalar=1.0, in1=bz[:, :], op0=ALU.add, op1=ALU.mult), t)
            banks.give(bz, t_sz)
            yield
            yield
            yield
            by, free = banks.take()
            for h in range(8):
                t = PE.op(lambda e, h=h: e.matmul(
                    by[64 * (h % 2):64 * (h % 2) + 64, (h // 2) * 128:(h // 2 + 1) * 128],
                    XH[ns][:, h * 64:h * 64 + 64], L[ns][:, h, :],
                    start=True, stop=True), t_m, t_xd, *free, last=(h == 7))
            L.read_by(ns, [t])
            XH.read_by(ns, [t])
            dtt.read_by(g, [t_xd])
            if ("scr", (ns + 1) // NB) in tok:
                fetch(ns + 1)
            yield
            t = DV.op(lambda e: e.tensor_tensor(Y[ns][:, :], by[:, :], DX[ns][:, :], ALU.add),
                      t, t_dx, *Y.readers(ns))
            DX.read_by(ns, [t])
            banks.give(by, t)
            t = GP.op(lambda e: e.tensor_tensor(Y[ns][:, :], Y[ns][:, :], SZ[ns][:, :], ALU.mult), t, t_sz)
            SZ.read_by(ns, [t])
            tok["y", ns] = t

        def second_half(ns):
            g, b = ns // NB, ns % NB
            st = stb[ns]
            t_y = tok["y", ns]
            t_sq2 = AC.op(lambda e: e.activation(SQ[ns][:, :, :], cv(Y[ns][:, :]), ACT.Square), t_y, *SQ.readers(ns))
            yield
            t = GP.op(lambda e: e.tensor_tensor(SQ[ns][:, 0:2, :], SQ[ns][:, 0:2, :], SQ[ns][:, 2:4, :], ALU.add), t_sq2)
            t_s2 = GP.op(lambda e: e.tensor_tensor(SQ[ns][:, 0, :], SQ[ns][:, 0, :], SQ[ns][:, 1, :], ALU.add), t)
            yield
            bo, free = banks.take()
            for k in range(4):
                PE.op(lambda e, k=k: e.matmul(bo[:, 0:256], Y[ns][:, k * 128:(k + 1) * 128], wout[:, k, :],
                                              start=(k == 0), stop=(k == 3)), t_y, t_wo2, *free, last=False)
            t_o = PE.op(lambda e: e.matmul(bo[:, 256:257], SQ[ns][:, 0, :], ones1[:, :], start=True, stop=True),
                        t_s2, t_one)
            SQ.read_by(ns, [t_o])
            Y.read_by(ns, [t_o])
            t = DV.op(lambda e: e.tensor_scalar(st[:, 1:2], bo[:, 256:257], 1.0 / 512, EPS, ALU.mult, ALU.add),
                      t_o, *stb.readers(ns))
            t_r2 = GP.op(lambda e: e.tensor_tensor(st[:, 1:2], st[:, 1:2], mhalf[:, :], ALU.pow), t, t_mh)
            yield
            hh = X2[g][:, b, :]
            t = DV.op(lambda e: e.scalar_tensor_tensor(
                out=hh, in0=bo[:, 0:256], scalar=st[:, 1:2], in1=X2[g][:, b, :], op0=ALU.mult, op1=ALU.add),
                t_o, t_r2)
            banks.give(bo, t)
            t = layer_stats(hh, st, 2, t)
            yield
            t = DV.op(lambda e: e.tensor_scalar(
                xh[ns][:, :], hh, st[:, 2:3], st[:, 3:4], ALU.subtract, ALU.mult), t, *xh.readers(ns))
            stb.read_by(ns, [t])
            yield
            yield
            hb, free = banks.take()
            t = turns(hb, lambda i: xh[ns][:, i * 128:(i + 1) * 128], 0, 2, t, *free)
            xh.read_by(ns, [t])
            t = AC.op(lambda e: e.activation(HT[g][:, :, b * 128:(b + 1) * 128], hb[:, 0:256].rearrange(
                "p (k t) -> p k t", k=2), ACT.Copy), t, *HT.readers(g))
            banks.give(hb, t)
            tok["h", g] = t

        def stream_b2(g):
            for b in range(NB):
                ns = g * NB + b
                halves = [first_half(ns)] if ns < NG * NB else []
                if ns >= 1 and ns - 1 < NG * NB:
                    halves.append(second_half(ns - 1))
                while halves:
                    for h in list(halves):
                        try:
                            next(h)
                        except StopIteration:
                            halves.remove(h)
                        yield

        qc = [0]

        def stream_c(g):
            t_k1, t_v = tok["ctx", g]
            for m in range(2):
                bk, t = project(wq1, HT[g], m, tok["h", g], t_wq1s)
                t_q = AC.op(lambda e, m=m, bk=bk: e.activation(Q1T[g][:, m, :], bk[:, 0:T], ACT.Identity,
                                                               bias=bq1[:, m:m + 1]), t, t_bq1, *Q1T.readers(g))
                banks.give(bk, t_q)
                yield
            HT.read_by(g, [t])
            exp_t, pt_t = {}, {}
            N = 4
            st = stc[g]
            for i in range(N + LTC + LA):
                if i < N:
                    n = qc[0] + i
                    bk, free = banks.take()
                    r3 = slice(32 * i, 32 * i + 3)
                    r = slice(32 * i, 32 * i + 32)
                    for q in range(4):
                        m, tt = q % 2, slice((q // 2) * 128, (q // 2 + 1) * 128)
                        t_s = PE.op(lambda e, bk=bk, q=q, m=m, tt=tt, r=r: e.matmul(
                            bk[:, q * 128:(q + 1) * 128], Q1T[g][r, m, tt], K1T[g][r, m, tt],
                            start=(q == 0), stop=False), t_q, t_k1, *free, last=False)
                    t_s = PE.op(lambda e, bk=bk, r3=r3: e.matmul(bk[:, :], onesb[r3, :], maskb[r3, :, :].rearrange(
                        "p a k -> p (a k)"), start=False, stop=True), t_mb, t_ones)
                    softmax_part(bk, t_s, PC_, n, st, 1.0, stc.readers(g) if i == 0 else [], 4 * i)
                    t_d = (DV.sem, DV.n)
                    yield
                if 1 <= i <= N:
                    n = qc[0] + i - 1
                    rc = st[:, 16 + 4 * (i - 1):20 + 4 * (i - 1)]
                    t = DV.op(lambda e, rc=rc: e.reciprocal(rc, rc), exp_t[i - 1])
                    exp_t[i - 1] = GP.op(lambda e, n=n, rc=rc: e.tensor_tensor(
                        PC_[n][:, :, :], PC_[n][:, :, :], rc.unsqueeze(2).to_broadcast([128, 4, 128]), ALU.mult), t)
                    if i == N:
                        stc.read_by(g, [exp_t[i - 1]])
                    yield
                if LTC <= i < N + LTC:
                    n = qc[0] + i - LTC
                    bk, free = banks.take()
                    P = PC_[n]
                    t = turns(bk, lambda q, P=P: P[:, q, :], 0, 4, exp_t[i - LTC], *free)
                    PC_.read_by(n, [t])
                    t = AC.op(lambda e, bk=bk, n=n: e.activation(PTC[n][:, :, :], bk[:, :].rearrange(
                        "p (i k) -> p i k", i=4), ACT.Copy), t, *PTC.readers(n))
                    banks.give(bk, t)
                    pt_t[i - LTC] = t
                    yield
                if i < N:
                    for q in range(4):
                        exp_t[i] = AC.op(lambda e, n=qc[0] + i, q=q, i=i: e.activation(
                            PC_[n][:, q, :], PC_[n][:, q, :], ACT.Exp, scale=32 ** -0.5,
                            accum_out=st[:, 16 + 4 * i + q:17 + 4 * i + q]), t_d)
                if i >= LTC + LA and (i - LTC - LA) % 2 == 1:
                    k = (i - LTC - LA) // 2
                    if k == 0:
                        o, free = banks.take()
                    for b in range(NB):
                        for m in range(2):
                            for j in (2 * k, 2 * k + 1):
                                c = 2 * m + j % 2
                                t_o = PE.op(lambda e, o=o, b=b, k=k, c=c, n=qc[0] + j, m=m: e.matmul(
                                    o[32 * c:32 * c + 32, (2 * b + k) * 128:(2 * b + k + 1) * 128],
                                    V1[g][:, b, 4 * k + c, :], PTC[n][:, 2 * b + m, :], start=True, stop=True),
                                    pt_t[j], t_v[b], *free, last=(b == 1 and c == 3))
                    for j in (2 * k, 2 * k + 1):
                        PTC.read_by(qc[0] + j, [t_o])
                    yield
            t_ot = AC.op(lambda e, o=o: e.activation(OT[g][:, :, :], o[:, :].rearrange("p (k t) -> p k t", k=4),
                                                     ACT.Copy), t_o, *OT.readers(g))
            banks.give(o, t_ot)
            yield
            yield
            bo, free = banks.take()
            for b in range(NB):
                for k in range(2):
                    t = PE.op(lambda e, bo=bo, b=b, k=k: e.matmul(
                        bo[:, b * 256:(b + 1) * 256], OT[g][:, 2 * b + k, :], wo[:, k, :],
                        start=(k == 0), stop=(k == 1)), t_ot, t_wo, *free, last=(b == 1 and k == 1))
            OT.read_by(g, [t])
            yield
            t_h = DV.op(lambda e, bo=bo: e.tensor_tensor(
                res[g][:, :, :], bo[:, :].rearrange("p (b c) -> p b c", b=NB), X2[g][:, :, :], ALU.add),
                t, *res.readers(g))
            banks.give(bo, t_h)
            t = dma(f"out{g % len(res.tiles)}", a["out"][g], res[g][:, :, :], t_h)
            res.read_by(g, [t])
            yield
            K1T.read_by(g, [t_s])
            Q1T.read_by(g, [t_s])
            V1.read_by(g, [t_o])
            X2.read_by(g, [t_h])
            qc[0] += N

        lags = ((stream_a1, 0, NG), (stream_a2, 1, NG), (stream_b1, 2, NG), (stream_b2, 3, NG + 1), (stream_c, 5, NG))
        for step in range(NG + 5):
            merge([f(step - lag) if 0 <= step - lag < n else None for f, lag, n in lags], SHARE, PHASE)
        SP.wait([(rec[0], rec[1]) for rec in dma_sems.values()])

        block = ctx.enter_context(nc.Block())
        block.tensor(PE.run)
        block.vector(DV.run)
        block.scalar(AC.run)
        block.gpsimd(GP.run)
        block.sync(SP.run)


def kernel(x, ctx_1024, mask_BxS2_ik0, mask_1xS2_bf0, **w):
    import numpy as np
    import concourse.bacc as bacc
    from concourse.bass_utils import run_bass_kernel_spmd

    w = {k: np.asarray(v) for k, v in w.items()}
    x, c = np.asarray(x), np.asarray(ctx_1024)

    def feature_major(v):
        return np.ascontiguousarray(v.reshape(NG, T, 2, 128).transpose(0, 3, 2, 1))

    def rows(v):
        return np.ascontiguousarray(v.reshape(-1, 128, v.shape[-1]).transpose(1, 0, 2))

    def cols(v):
        return v.reshape(-1, 128).T

    p = np.arange(128)
    pcols = np.zeros((128, 20), np.float32)
    for at, n, name in ((4, 2, "L1_xattn_m_norm_w"),
                        (6, 4, "L1_xattn_gnorm_w"), (10, 2, "L1_xattn_ca_ln_w"), (12, 2, "L1_xattn_ca_ln_b")):
        pcols[:, at:at + n] = cols(w[name])
    pcols[:, 14:18] = cols(np.repeat(w["L1_xattn_D_skip"], 64))
    order = np.concatenate([16 * (4 * j + 2 * m + e) + np.arange(16)
                            for m in range(2) for j in range(4) for e in range(2)])
    pcols[:, 0:2], pcols[:, 2:4] = cols(w["L0_xattn_bq"][order]), cols(w["L0_xattn_bk"][order])
    order1 = np.concatenate([32 * (4 * k + 2 * m + i) + np.arange(32)
                             for m in range(2) for k in range(2) for i in range(2)])
    arrays = {
        "ident": np.eye(128, dtype=np.float32),
        "par": np.stack([(p // 16 + 1) % 2, (p // 16) % 2], 1).astype(np.float32),
        "sel": np.stack([p % 32 == i for i in range(3)], 1).astype(np.float32),
        "pcols": pcols,
        "convp": np.ascontiguousarray(np.concatenate(
            [w["L1_xattn_conv_w"].reshape(6, 128, 4), w["L1_xattn_conv_b"].reshape(6, 128, 1)], 2).transpose(1, 0, 2)),
        "heads": np.concatenate([w["L1_xattn_dt_bias"], w["L1_xattn_A_log"]])[None],
        "maskT": np.ascontiguousarray(np.asarray(mask_BxS2_ik0).T),
        "pad": np.asarray(mask_1xS2_bf0),
        "xT": feature_major(x), "cT": feature_major(c),
        "xt": np.ascontiguousarray(x.reshape(NG, NB, S, D).transpose(0, 2, 1, 3)),
        "wq": rows(w["L0_xattn_Wq"][:, order]), "wk": rows(w["L0_xattn_Wk"][:, order]),
        "wv": rows(np.concatenate([w["L0_xattn_Wv"], w["L1_xattn_Wv"]], 1)),
        "wk1": rows(w["L1_xattn_Wk"][:, order1]), "wq1": rows(w["L1_xattn_Wq"][:, order1]), "wo": rows(w["L1_xattn_Wo"]),
        "win": rows(w["L1_xattn_in_proj_w"]), "wout": rows(w["L1_xattn_out_proj_w"]),
        "bv": w["L0_xattn_bv"], "gamma": w["L0_xattn_gamma"], "beta": w["L0_xattn_beta"],
    }
    nc = bacc.Bacc("TRN2", target_bir_lowering=False, num_devices=1)
    args, ins = {}, {}
    for name, v in arrays.items():
        ins["in_" + name] = v
        args[name] = nc.dram_tensor("in_" + name, v.shape, mybir.dt.from_np(v.dtype), kind="ExternalInput").ap()
    args["out"] = nc.dram_tensor("out_x", (NG, S, NB, D), F32, kind="ExternalOutput").ap()
    program(nc, args)
    r = run_bass_kernel_spmd(nc, [ins], core_ids=[0])
    out = r.results[0]["out_x"]
    return np.ascontiguousarray(out.transpose(0, 2, 1, 3)).reshape(NG * NB, S, D)
```

```python
from contextlib import ExitStack

import concourse.bass as bass
from concourse import mybir

F32 = mybir.dt.float32
F32R = mybir.dt.float32r
BF16 = mybir.dt.bfloat16
ALU = mybir.AluOpType
ACT = mybir.ActivationFunctionType
AX_X = mybir.AxisListType.X

NG = 32
NB = 2
S = 128
D = 256
T = NB * S
EPS = 1e-5
LT = 3
LTC = 4
LN = 2
LA = 2
BIG = 3.0e38
NPROJ = 1288
SHARE = (5.4, 31.0, 26.7, 36.8, 19.2, 4)
PHASE = (-1.3, 0.5, 0.15, 3.0, 0.5, 1.8)


class Engine:

    def __init__(self, sem):
        self.sem, self.n, self.q, self.met = sem, 0, [], {}

    def wait(self, tokens):
        for sem, value in tokens:
            if self.met.get(id(sem), 0) < value:
                self.met[id(sem)] = value
                self.q.append(lambda e, s=sem, v=value: e.wait_ge(s, v))

    def op(self, fn, *tokens, last=True):
        self.wait(tokens)
        if not last:
            self.q.append(fn)
            return None
        self.n += 1
        self.q.append(lambda e: fn(e).then_inc(self.sem, 1))
        return (self.sem, self.n)

    def run(self, e):
        for f in self.q:
            f(e)


class Banks:

    def __init__(self, tiles):
        self.idle = [(t, None) for t in tiles]

    def take(self):
        tile, token = self.idle.pop(0)
        return tile, ([token] if token else [])

    def give(self, tile, token):
        self.idle.append((tile, token))


class Slots:

    def __init__(self, tiles):
        self.tiles, self.free = tiles, [[] for _ in tiles]

    def __getitem__(self, i):
        return self.tiles[i % len(self.tiles)]

    def readers(self, i):
        return self.free[i % len(self.tiles)]

    def read_by(self, i, tokens):
        self.free[i % len(self.tiles)] = list(tokens)


def merge(streams, weights, phases):
    done = [0] * len(streams)
    live = [s is not None for s in streams]
    while any(live):
        i = min((k for k in range(len(streams)) if live[k]), key=lambda k: (done[k] + phases[k]) / weights[k])
        try:
            next(streams[i])
            done[i] += 1
        except StopIteration:
            live[i] = False
    return done


def program(nc, a):
    with ExitStack() as ctx:
        def sb(name, shape, dt=F32):
            return ctx.enter_context(nc.sbuf_tensor(name, shape, dt))

        def sem(name):
            return ctx.enter_context(nc.semaphore(name))

        def slots(name, n, shape, dt=F32):
            return Slots([sb(f"{name}{i}", shape, dt) for i in range(n)])

        PE, DV, AC, GP, SP = (Engine(sem(f"s_{n}")) for n in ("pe", "dve", "act", "pool", "sp"))
        banks = Banks([ctx.enter_context(nc.psum_tensor(f"bank{i}", [128, 512], F32)) for i in range(8)])
        dma_sems = {}

        def dma(name, out, in_, *tokens):
            if name not in dma_sems:
                dma_sems[name] = [sem("d_" + name), 0]
            rec = dma_sems[name]
            SP.wait(tokens)
            if rec[1]:
                SP.wait([(rec[0], rec[1])])
            rec[1] += 16
            SP.q.append(lambda e, s=rec[0]: e.dma_start(out, in_).then_inc(s, 16))
            return (rec[0], rec[1])

        ident = sb("ident", [128, 128])
        id8 = sb("id8", [128, 8, 128], BF16)
        par = sb("par", [128, 2])
        sel = sb("sel", [128, 3])
        onesb = sb("onesb", [128, 128], BF16)
        wqh, wql = (sb(n, [128, 2, 256], F32R) for n in ("wqh", "wql"))
        wkh, wkl = (sb(n, [128, 2, 256], F32R) for n in ("wkh", "wkl"))
        wvh, wvl = (sb(n, [128, 2, 256], F32R) for n in ("wvh", "wvl"))
        wv1 = sb("wv1", [128, 2, 256])
        wk1 = sb("wk1", [128, 2, 256])
        wq1 = sb("wq1", [128, 2, 256])
        wo = sb("wo", [128, 2, 256])
        wnh = sb("wnh", [128, 2, 1280], F32R)
        wnl = sb("wnl", [128, 2, 1280], F32R)
        wdt = sb("wdt", [128, 2, 2, 16], F32R)
        wout = sb("wout", [128, 4, 256])
        pc = sb("pc", [128, 20])
        cw = sb("cw", [128, 6, 5])
        gam = sb("gam", [128, 256])
        bet = sb("bet", [128, 256])
        h8 = sb("h8", [128, 2, 8])
        negA = sb("negA", [128, 8])
        mrow = sb("mrow", [128, 128], mybir.dt.uint8)
        mi = sb("mi", [128, 64], mybir.dt.int32)
        sq = sb("sq", [128, 64])
        keep = sb("keep", [128, 128])
        maskb = sb("maskb", [128, 4, 128], BF16)
        vbias = sb("vbias", [128, 256], BF16)
        mhalf = sb("mhalf", [128, 1])
        ones1 = sb("ones1", [128, 1])
        kb = sb("kb", [128, 2, 2])
        bq1 = sb("bq1", [128, 2])

        xT = slots("xT", 1, [128, 2, T])
        cT = slots("cT", 1, [128, 2, T])
        xH = slots("xH", 1, [128, 2, T], F32R)
        xL = slots("xL", 1, [128, 2, T], F32R)
        cH = slots("cH", 1, [128, 2, T], F32R)
        cL = slots("cL", 1, [128, 2, T], F32R)
        cU = slots("cU", 1, [128, 2, T])
        xt = slots("xt", 1, [128, NB, D])
        OA = slots("OA", 1, [128, 512])
        QT = slots("QT", 2, [128, 2, T])
        KT = slots("KT", 2, [128, 2, NB, 2, 128])
        V0 = slots("V0", 2, [128, NB * 272 + 15])
        K1T = slots("K1T", 2, [128, 2, T])
        V1 = slots("V1", 2, [128, NB, 8, 32])
        PA = slots("PA", LT + 1, [128, 4, 128])
        PTA = slots("PTA", LA + 1, [128, 4, 128])
        PC_ = slots("PC", LTC + 1, [128, 4, 128])
        PTC = slots("PTC", LA + 2, [128, 4, 128])
        X2 = slots("X2", 5, [128, NB, D])
        sta = slots("sta", 4, [128, 48])
        stb = slots("stb", 4, [128, 16])
        stn = slots("stn", 4, [128, 1])
        stc = slots("stc", 4, [128, 32])
        xa = slots("xa", 2, [128, 256])
        xn = slots("xn", 2, [128, 256])
        xnT = slots("xnT", 2, [128, 2, T], F32R)
        xnL = slots("xnL", 2, [128, 2, T], F32R)
        XP = slots("XP", 3, [128, NB, 131])
        ACC = slots("ACC", 3, [128, NB, 128])
        XC = slots("XC", 2, [128, 6, T])
        SZ = slots("SZ", 1, [128, 4, T])
        dts = sb("dts", [128, 8, 8 * NB])
        dtt = slots("dtt", 3, [128, 8 * NB])
        decT = slots("decT", 2, [8 * NB, 128])
        DB = slots("DB", 2, [128, 1024])
        L = slots("L", 1, [128, 8, 128])
        XH = slots("XH", 1, [128, 512])
        DX = slots("DX", 1, [128, 512])
        Y = slots("Y", 2, [128, 512])
        SQ = slots("SQ", 1, [128, 4, 128])
        xh = slots("xh", 2, [128, 256])
        HT = slots("HT", 2, [128, 2, T])
        Q1T = slots("Q1T", 1, [128, 2, T])
        OT = slots("OT", 1, [128, 4, 128])
        junk = sb("junk", [128, 256], BF16)
        scratch = nc.dram_tensor("dec_scratch", [NG, NB * 8 * 128], F32, kind="Internal").ap()

        bvr, negm = xa[0], xa[1][:, 0:128]
        s0, s1, s2 = SQ[0][:, 0:2, :], SQ[0][:, 2, :].bitcast(BF16), Y[1][:, 0:256]
        s0 = s0.rearrange("p a b -> p (a b)")

        def bcast(v, n):
            return v.rearrange("(a n) -> a n", a=1).to_broadcast([128, n])

        consts = dma("c_id", ident[:, :], a["ident"])
        t_sel = dma("c_sel", sel[:, :], a["sel"])
        t_par = dma("c_par", par[:, :], a["par"])
        t_pc = dma("c_pc", pc[:, :], a["pcols"])
        t_cw = dma("c_cw", cw[:, :, :], a["convp"])
        t_mi = dma("c_mi", mi[:, :], a["maskT"])
        def halves(ring):
            return ring[0][:, :].rearrange("p (k c) -> p k c", k=2)

        wq_f, wk_f, wv_f = halves(Y), halves(DX), halves(XH)
        t_w = [dma("w_" + n, t, a[n]) for n, t in (("wq", wq_f), ("wk", wk_f), ("wv", wv_f))]

        loads = {}

        def load(name, ring, g, src=None):
            if g < NG:
                loads[name, g] = dma(f"{name}{g % len(ring.tiles)}", ring[g][:, :, :], a[src or name][g], *ring.readers(g))

        load("xT", xT, 0)
        load("cT", cT, 0)
        load("xt", xt, 0)
        t_h8 = dma("c_h8", h8[:, :, :], a["heads"].rearrange("a (b c) -> a b c", b=2).to_broadcast([128, 2, 8]))
        t_bv = dma("c_bv", bvr[:, :], bcast(a["bv"], 256))
        t_mr = dma("c_mr", mrow[:, :], a["pad"].to_broadcast([128, 128]))
        t_gam = dma("c_gam", gam[:, :], bcast(a["gamma"], 256))
        t_bet = dma("c_bet", bet[:, :], bcast(a["beta"], 256))
        stage = [XC[k][:, :, :].rearrange("p c t -> p (c t)")[:, 0:NPROJ] for k in range(2)]
        t_win = [dma(f"w_win{k}", stage[k], a["win"][:, k, :]) for k in range(2)]
        t_w.append(dma("w_wk1", wk1[:, :, :], a["wk1"]))
        t_w.append(dma("w_wv1", wv1[:, :, :], a["wv1"]))
        t_wout = dma("w_wout", wout[:, :, :], a["wout"])
        t_wq1 = dma("w_wq1", wq1[:, :, :], a["wq1"])
        t_wo = dma("w_wo", wo[:, :, :], a["wo"])
        load("cU", cU, 0, "cT")

        def v0(g):
            return V0[g][:, 0:NB * 272].rearrange("p (h d) -> p h d", d=17)

        t_ones = GP.op(lambda e: e.memset(onesb[:, :], 1.0))
        t_mh = GP.op(lambda e: e.memset(mhalf[:, :], -0.5))
        t_one = GP.op(lambda e: e.memset(ones1[:, :], 1.0))
        t_pad = []
        for i in range(3):
            t_pad.append(GP.op(lambda e, i=i: e.memset(XP[i][:, :, 0:3], 0.0)))
        for i in range(2):
            t_pad.append(GP.op(lambda e, i=i: e.memset(decT[i][:, 0:1], 0.0)))
            t_pad.append(GP.op(lambda e, i=i: e.memset(V0[i][:, NB * 272:], 0.0)))
            t_pad.append(GP.op(lambda e, i=i: e.memset(v0(i)[:, :, 16:17], 1.0)))
        t_sq = DV.op(lambda e: e.tensor_scalar(sq[:, :], mi[:, :], 0.0, 0.25, ALU.not_equal, ALU.mult), t_mi)
        t_kb = DV.op(lambda e: e.tensor_scalar(kb[:, 0, :], pc[:, 2:4], par[:, 0:1], None, ALU.mult), t_pc, t_par)
        t_k1 = DV.op(lambda e: e.tensor_scalar(s0[:, 0:1], par[:, 0:1], -BIG, None, ALU.mult), t_par)
        t_kb1 = DV.op(lambda e: e.tensor_scalar(kb[:, 1, :], pc[:, 2:4], s0[:, 0:1], None, ALU.add), t_k1)
        t_keep = DV.op(lambda e: e.tensor_scalar(keep[:, :], mrow[:, :], 0.0, None, ALU.is_equal), t_mr)
        t_neg = DV.op(lambda e: e.tensor_scalar(negm[:, :], mrow[:, :], 0.0, -1.0e9 * 32 ** 0.5,
                                                ALU.not_equal, ALU.mult), t_mr)

        def split2(src, hi, lo, *tokens):
            t = DV.op(lambda e: e.tensor_copy(hi, src), *tokens)
            return t, GP.op(lambda e: e.tensor_tensor(lo, src, hi.bitcast(F32), ALU.subtract), t)

        def split_in(name, ring, hi, lo, g):
            if g < NG:
                tok[name, g] = split2(ring[g][:, :, :], hi[g][:, :, :], lo[g][:, :, :], loads[name, g], *hi.readers(g))
                ring.read_by(g, tok[name, g])
                load(name, ring, g + 1)

        t_wkv = []
        for ring, f, hi, lo, t in ((Y, wq_f, wqh, wql, t_w[0]), (DX, wk_f, wkh, wkl, t_w[1]), (XH, wv_f, wvh, wvl, t_w[2])):
            t_wkv += split2(f, hi[:, :, :], lo[:, :, :], t)
            ring.read_by(0, t_wkv[-2:])
        tok = {}
        split_in("xT", xT, xH, xL, 0)
        split_in("cT", cT, cH, cL, 0)

        t_id8 = [GP.op(lambda e, h=h: e.tensor_copy(id8[:, h, :], ident[:, :]), consts) for h in range(8)][-1]

        def split3(src, n, dst, token):
            t = DV.op(lambda e: e.tensor_copy(s1[:, 0:n], src), token, t_sel)
            p = DV.op(lambda e: e.tensor_scalar(s0[:, 0:n], s1[:, 0:n], sel[:, 0:1], None, ALU.mult), t)
            r = DV.op(lambda e: e.tensor_tensor(s2[:, 0:n], src, s1[:, 0:n], ALU.subtract), t)
            for i in (1, 2):
                t = DV.op(lambda e: e.tensor_copy(s1[:, 0:n], s2[:, 0:n]), r, p)
                p = DV.op(lambda e, i=i: e.scalar_tensor_tensor(out=s0[:, 0:n], in0=s1[:, 0:n], scalar=sel[:, i:i + 1],
                                                                in1=s0[:, 0:n], op0=ALU.mult, op1=ALU.add), t, p)
                r = DV.op(lambda e: e.tensor_tensor(s2[:, 0:n], s2[:, 0:n], s1[:, 0:n], ALU.subtract), t)
            return DV.op(lambda e: e.tensor_copy(dst, s0[:, 0:n]), p, r)

        t_vb = split3(bvr[:, :], 256, vbias[:, :], t_bv)
        t_mb = split3(negm[:, :], 128, maskb[:, 0, :], t_neg)
        xa.read_by(0, [t_vb])
        xa.read_by(1, [t_mb])
        for i in range(1, 4):
            t_mb = DV.op(lambda e, i=i: e.tensor_copy(maskb[:, i, :], maskb[:, 0, :]), t_mb)
        t_split = []
        for k in range(2):
            t_wz = []
            for lo, hi, c in ((0, 512, 0.5), (512, NPROJ, 1.0)):
                t_wz.append(GP.op(lambda e, k=k, lo=lo, hi=hi, c=c: e.tensor_scalar(
                    stage[k][:, lo:hi], stage[k][:, lo:hi], pc[:, 4 + k:5 + k], c, ALU.mult, ALU.mult), t_win[k], t_pc))
            t_hi = DV.op(lambda e, k=k: e.tensor_copy(wnh[:, k, :], stage[k][:, 0:1280]), *t_wz)
            t_lo = DV.op(lambda e, k=k: e.tensor_tensor(wnl[:, k, :], stage[k][:, 0:1280], wnh[:, k, :].bitcast(F32),
                                                        ALU.subtract), t_hi)
            for i in range(2):
                t_wd = DV.op(lambda e, k=k, i=i: e.tensor_copy(wdt[:, k, i, 0:8], stage[k][:, 1280:1288]), *t_wz)
            t_wd = DV.op(lambda e, k=k: e.tensor_tensor(
                wdt[:, k, 0, 8:16], stage[k][:, 1280:1288], wdt[:, k, 0, 0:8].bitcast(F32), ALU.subtract), t_wd)
            DV.op(lambda e, k=k: e.tensor_scalar(wdt[:, k, 1, 8:16], stage[k][:, 1280:1288], 0.0, None, ALU.mult),
                  t_wd)
            XC.read_by(k, [t_lo, (DV.sem, DV.n)])
            t_split.append((DV.sem, DV.n))
        t_wz = t_split[-1]
        for k in range(4):
            t_wo2 = GP.op(lambda e, k=k: e.tensor_scalar(
                wout[:, k, :], wout[:, k, :], pc[:, 6 + k:7 + k], None, ALU.mult), t_wout, t_pc)
        t_cw2 = GP.op(lambda e: e.tensor_scalar(cw[:, :, :], cw[:, :, :], 0.5, None, ALU.mult), t_cw)
        t_ea = AC.op(lambda e: e.activation(negA[:, :], h8[:, 1, :], ACT.Exp), t_h8)
        t_nA = DV.op(lambda e: e.tensor_scalar(negA[:, :], negA[:, :], -1.0, None, ALU.mult), t_ea)

        def setup_wq1():
            bk, w = banks.take()
            for m in range(2):
                for k in range(2):
                    t_b1 = PE.op(lambda e, m=m, k=k: e.matmul(bk[:, m:m + 1], wq1[:, k, m * 128:(m + 1) * 128],
                                                              pc[:, 12 + k:13 + k], start=(k == 0), stop=(k == 1)),
                                 t_wq1, t_pc, *w)
            t_bq1 = DV.op(lambda e: e.tensor_copy(bq1[:, :], bk[:, 0:2]), t_b1)
            banks.give(bk, t_bq1)
            for k in range(2):
                t_wq1s = GP.op(lambda e, k=k: e.tensor_scalar(wq1[:, k, :], wq1[:, k, :], pc[:, 10 + k:11 + k], None,
                                                              ALU.mult), t_b1)
            tok["wq1"] = t_wq1s, t_bq1

        def project(w_ap, src, m, *tokens):
            bk, free = banks.take()
            for k in range(2):
                t = PE.op(lambda e, k=k: e.matmul(bk[:, 0:T], w_ap[:, k, m * 128:(m + 1) * 128], src[:, k, :],
                                                  start=(k == 0), stop=(k == 1)), *tokens, *free, last=(k == 1))
            return bk, t

        def project3(bk, at, col, g, last):
            _, free = at
            passes = [(k, w, x) for k in range(2) for w, x in ((wnl, xnT[g]), (wnh, xnL[g]), (wnh, xnT[g]))]
            for n, (k, w, x) in enumerate(passes):
                t = PE.op(lambda e, k=k, w=w, x=x, n=n: e.matmul(
                    bk[:, col[1]:col[1] + T], w[:, k, col[0]:col[0] + 128], x[:, k, :],
                    start=(n == 0), stop=(n == 5)), tok["xnT", g], t_wz, *free, last=(last and n == 5))
            return t

        def turns(bk, src, col, n, *tokens, last=True):
            for i in range(n):
                t = PE.op(lambda e, i=i: e.transpose(bk[:, col + i * 128:col + (i + 1) * 128], src(i), ident[:, :]),
                          *tokens, consts, last=(last and i == n - 1))
            return t

        def softmax_part(bk, t_s, ring, n, st, scale, tokens, mcol):
            P = ring[n]
            v = bk[:, :].rearrange("p (i k) -> p i k", i=4)
            mx = st[:, mcol:mcol + 4]
            t_m = DV.op(lambda e: e.tensor_reduce(mx, v, AX_X, ALU.max), t_s, *tokens)
            t_d = DV.op(lambda e: e.tensor_tensor(P[:, :, :], v, mx.unsqueeze(2).to_broadcast([128, 4, 128]),
                                                  ALU.subtract), t_m, *ring.readers(n))
            banks.give(bk, t_d)
            return lambda: AC.op(lambda e: e.activation(P[:, :, :], P[:, :, :], ACT.Exp, scale=scale), t_d)

        def layer_stats(src, st, c, token, *more):
            t = DV.op(lambda e: e.bn_stats(st[:, c + 2:c + 8], src), token, *more)
            t = DV.op(lambda e: e.bn_aggr(st[:, c:c + 2], st[:, c + 2:c + 8]), t)
            t = GP.op(lambda e: e.tensor_scalar(st[:, c + 1:c + 2], st[:, c + 1:c + 2], EPS, None, ALU.add), t)
            return GP.op(lambda e: e.tensor_tensor(st[:, c + 1:c + 2], st[:, c + 1:c + 2], mhalf[:, :], ALU.pow), t, t_mh)

        qa = [0]

        def stream_a1(g):
            t_x, t_c = tok["xT", g], tok["cT", g]

            def project2(wh, wl, hi, lo, m, *tokens):
                bk, free = banks.take()
                for n, (k, w, x) in enumerate((k, w, x) for k in range(2) for w, x in ((wl, hi), (wh, lo), (wh, hi))):
                    t = PE.op(lambda e, bk=bk, m=m, k=k, w=w, x=x, n=n: e.matmul(
                        bk[:, 0:T], w[:, k, m * 128:(m + 1) * 128], x[g][:, k, :], start=(n == 0), stop=(n == 5)),
                        *tokens, *t_wkv, *free, last=(n == 5))
                return bk, t

            for m in range(2):
                bk, t = project2(wqh, wql, xH, xL, m, *t_x)
                t_q = AC.op(lambda e, m=m, bk=bk: e.activation(QT[g][:, m, :], bk[:, 0:T], ACT.Relu, bias=pc[:, m:m + 1]),
                            t, t_pc, *QT.readers(g))
                banks.give(bk, t_q)
                yield
            xH.read_by(g, [t])
            for m in range(2):
                bk, t = project2(wkh, wkl, cH, cL, m, *t_c)
                v = bk[:, 0:T].rearrange("p (b k) -> p b k", b=NB)
                t_k = AC.op(lambda e, m=m, v=v: e.activation(KT[g][:, m, :, 0, :], v, ACT.Relu, bias=kb[:, 0, m:m + 1],
                                                             scale=par[:, 0:1]), t, t_kb, t_par, *KT.readers(g))
                t_k2 = DV.op(lambda e, m=m, v=v: e.tensor_scalar(KT[g][:, m, :, 1, :], v, kb[:, 1, m:m + 1], 0.0,
                                                                 ALU.add, ALU.max), t_k, t_kb1, *KT.readers(g))
                banks.give(bk, t_k2)
                yield
            bk, free = banks.take()
            for b in range(NB):
                PE.op(lambda e, b=b: e.matmul(bk[:, b * 256:(b + 1) * 256], onesb[0:3, :], vbias[0:3, :],
                                              start=True, stop=False), t_ones, t_vb, *free, last=False)
                for n, (k, w, c) in enumerate((k, w, c) for k in range(2)
                                              for w, c in ((wvl, cH), (wvh, cL), (wvh, cH))):
                    t = PE.op(lambda e, k=k, b=b, w=w, c=c, n=n: e.matmul(
                        bk[:, b * 256:(b + 1) * 256], c[g][:, k, b * 128:(b + 1) * 128], w[:, k, :],
                        start=False, stop=(n == 5)), last=(b == NB - 1 and n == 5))
            t_v = AC.op(lambda e: e.activation(
                v0(g)[:, :, 0:16], bk[:, :].rearrange("p (h d) -> p h d", d=16), ACT.Relu),
                t, *t_pad, *V0.readers(g))
            banks.give(bk, t_v)
            yield
            cH.read_by(g, [t])
            split_in("xT", xT, xH, xL, g + 1)
            split_in("cT", cT, cH, cL, g + 1)
            tok["qkv", g] = (t_q, t_k, t_k2, t_v)

        def stream_k(g):
            t_c = loads["cU", g]
            for m in range(2):
                bk, t = project(wk1, cU[g], m, t_c, t_w[3])
                v = bk[:, 0:T].rearrange("p (b k) -> p b k", b=NB)
                t_k1 = DV.op(lambda e, m=m, v=v: e.tensor_tensor(
                    K1T[g][:, m, :].rearrange("p (b k) -> p b k", b=NB), v,
                    keep[:, :].unsqueeze(1).to_broadcast([128, NB, 128]), ALU.mult), t, t_keep, *K1T.readers(g))
                banks.give(bk, t_k1)
                yield
            bk, free = banks.take()
            for b in range(NB):
                for k in range(2):
                    t = PE.op(lambda e, k=k, b=b: e.matmul(
                        bk[:, b * 256:(b + 1) * 256], cU[g][:, k, b * 128:(b + 1) * 128], wv1[:, k, :],
                        start=(k == 0), stop=(k == 1)), t_w[4], *free, last=(b == NB - 1 and k == 1))
            t_v = AC.op(lambda e: e.activation(
                V1[g][:, :, :, :], bk[:, :].rearrange("p (b h d) -> p b h d", b=NB, h=8), ACT.Copy),
                t, *V1.readers(g))
            banks.give(bk, t_v)
            cU.read_by(g, [t])
            load("cU", cU, g + 1, "cT")
            tok["ctx", g] = (t_k1, t_v)
            yield

        def stream_a2(g):
            t_q, t_k, t_k2, t_v = tok["qkv", g]
            t_xt = loads["xt", g]

            units = [(b, j) for b in range(NB) for j in range(4)]
            exp_t, pt_t, av, tails = {}, {}, {}, []
            N = len(units)

            def finish(b, o, t):
                ns = g * NB + b
                st = sta[ns]
                xv = xa[ns][:, :].rearrange("p (h d) -> p h d", h=16)
                t = AC.op(lambda e: e.activation(OA[ns][:, :], o[:, :], ACT.Copy), t, *OA.readers(ns))
                banks.give(o, t)
                yield 1
                ot, free = banks.take()
                t = turns(ot, lambda i: OA[ns][:, i * 128:(i + 1) * 128], 0, 4, t, *free)
                OA.read_by(ns, [t])
                ov = ot[:, :].rearrange("p (h d) -> p h d", h=16)
                yield 1
                t = DV.op(lambda e: e.reciprocal(st[:, 16:32].unsqueeze(2), ov[:, :, 16:17]), t)
                t = DV.op(lambda e: e.tensor_tensor(
                    xv, ov[:, :, 0:16], st[:, 16:32].unsqueeze(2).to_broadcast([128, 16, 16]), ALU.mult),
                    t, *xa.readers(ns))
                banks.give(ot, t)
                t = GP.op(lambda e: e.tensor_tensor(xa[ns][:, :], xa[ns][:, :], xt[g][:, b, :], ALU.add), t, t_xt)
                xt.read_by(g, [t])
                yield 1
                t = layer_stats(xa[ns][:, :], st, 32, t)
                yield 1
                t = DV.op(lambda e: e.tensor_scalar(
                    xa[ns][:, :], xa[ns][:, :], st[:, 32:33], st[:, 33:34], ALU.subtract, ALU.mult), t)
                sta.read_by(ns, [t])
                x2 = X2[g][:, b, :]
                t = GP.op(lambda e: e.tensor_tensor(x2, xa[ns][:, :], gam[:, :], ALU.mult), t, t_gam, *X2.readers(g))
                xa.read_by(ns, [t])
                tok["x2", g, b] = GP.op(lambda e: e.tensor_tensor(x2, x2, bet[:, :], ALU.add), t, t_bet)

            for i in range(N + LT + LA):
                if i < N:
                    b, j = units[i]
                    n = qa[0] + i
                    bk, free = banks.take()
                    r = slice(32 * j, 32 * j + 32)
                    for m in range(2):
                        t_s = PE.op(lambda e, bk=bk, m=m, b=b, r=r: e.matmul(
                            bk[:, m * 256:(m + 1) * 256], QT[g][r, m, b * 128:(b + 1) * 128], KT[g][r, m, b, :, :],
                            start=True, stop=True), t_q, t_k, t_k2, *free, last=(m == 1))
                    ns = g * NB + b
                    late_exp = softmax_part(bk, t_s, PA, n, sta[ns], sq[:, ns:ns + 1],
                                            [t_sq, *(sta.readers(ns) if j == 0 else [])], 4 * j)
                    yield
                if LT <= i < N + LT:
                    b, j = units[i - LT]
                    n = qa[0] + i - LT
                    bk, free = banks.take()
                    P = PA[n]
                    t = turns(bk, lambda q, P=P: P[:, q, :], 0, 4, exp_t[i - LT], *free)
                    PA.read_by(n, [t])
                    t = AC.op(lambda e, bk=bk, n=n: e.activation(PTA[n][:, :, :], bk[:, :].rearrange(
                        "p (i k) -> p i k", i=4), ACT.Copy), t, *PTA.readers(n))
                    banks.give(bk, t)
                    pt_t[i - LT] = t
                    yield
                if i < N:
                    exp_t[i] = late_exp()
                if LT + LA <= i:
                    b, j = units[i - LT - LA]
                    n = qa[0] + i - LT - LA
                    if j == 0:
                        av[b] = banks.take()
                    o, free = av[b]
                    for q in range(4):
                        t = PE.op(lambda e, o=o, n=n, q=q, b=b, j=j: e.matmul(
                            o[32 * q:32 * q + 32, j * 128:(j + 1) * 128], V0[g][:, 272 * b + 17 * (4 * j + q):272 * b + 17 * (4 * j + q) + 32],
                            PTA[n][:, q, :], start=True, stop=True),
                            pt_t[i - LT - LA], t_v, *free, last=(q == 3))
                    PTA.read_by(n, [t])
                    t_last = t
                    if j == 3:
                        tails.append(finish(b, o, t))
                    yield
                for tail in list(tails):
                    if next(tail, 0) == 0:
                        tails.remove(tail)
            while tails:
                yield
                yield
                yield
                if next(tails[0], 0) == 0:
                    tails.pop(0)
            load("xt", xt, g + 1)
            QT.read_by(g, [t_s])
            KT.read_by(g, [t_s])
            V0.read_by(g, [t_last])
            qa[0] += N

        def stream_b1(g):
            t_r = []
            for b in range(NB):
                ns = g * NB + b
                x2 = X2[g][:, b, :]
                t = AC.op(lambda e, x2=x2, ns=ns: e.activation(junk[:, 0:256], x2, ACT.Square, scale=1.0 / 16,
                                                               accum_out=stn[ns][:, 0:1]),
                          tok["x2", g, b], (AC.sem, AC.n), *stn.readers(ns))
                t = GP.op(lambda e, ns=ns: e.tensor_scalar(stn[ns][:, :], stn[ns][:, :], EPS, None, ALU.add), t)
                t_r.append(GP.op(lambda e, ns=ns: e.tensor_tensor(stn[ns][:, :], stn[ns][:, :], mhalf[:, :], ALU.pow),
                                 t, t_mh))
                yield
            t_n = []
            for b in range(NB):
                ns = g * NB + b
                t = DV.op(lambda e, ns=ns, b=b: e.tensor_scalar(xn[ns][:, :], X2[g][:, b, :], stn[ns][:, 0:1], None,
                                                                ALU.mult), t_r[b], *xn.readers(ns))
                stn.read_by(ns, [t])
                t_n.append(t)
            yield
            yield
            bk, free = banks.take()
            for b in range(NB):
                ns = g * NB + b
                t = turns(bk, lambda i, ns=ns: xn[ns][:, i * 128:(i + 1) * 128], b * 256, 2, t_n[b], *free)
                xn.read_by(ns, [t])
            v = bk[:, :].rearrange("p (b k t) -> p k b t", b=NB, k=2)
            o = xnT[g][:, :, :].rearrange("p k (b t) -> p k b t", b=NB)
            ol = xnL[g][:, :, :].rearrange("p k (b t) -> p k b t", b=NB)
            for k in range(2):
                t = AC.op(lambda e, v=v, o=o, k=k: e.activation(o[:, k], v[:, k], ACT.Copy), t, *xnT.readers(g))
            for k in range(2):
                t = DV.op(lambda e, v=v, o=o, ol=ol, k=k: e.tensor_tensor(
                    ol[:, k], v[:, k], o[:, k].bitcast(F32), ALU.subtract), t, *xnL.readers(g))
            banks.give(bk, t)
            t_n = t
            tok["xnT", g] = t
            yield
            yield

            d = [dts[:, i, :] for i in range(8)]
            dt = dtt[g][:, :]
            v4 = lambda x: x.rearrange("p (b h) -> p b h", b=NB)
            bc = lambda x: x.unsqueeze(1).to_broadcast([128, NB, 8])

            def steps():
                bk, free = banks.take()
                for b in range(NB):
                    for n, (k, i, x) in enumerate((k, i, x) for k in range(2) for i, x in enumerate((xnT[g], xnL[g]))):
                        t = PE.op(lambda e, bk=bk, k=k, b=b, i=i, x=x, n=n: e.matmul(
                            bk[:, b * 16:b * 16 + 16], x[:, k, b * 128:(b + 1) * 128], wdt[:, k, i, :],
                            start=(n == 0), stop=(n == 3)), t_n, t_wz, *free, last=(b == NB - 1 and n == 3))
                vv = bk[:, 0:16 * NB].rearrange("p (b i h) -> p b i h", b=NB, i=2)
                t = DV.op(lambda e: e.tensor_tensor(v4(d[0]), vv[:, :, 1, :], bc(h8[:, 0, :]), ALU.add), t, t_h8,
                          *tok.get("dts", []))
                t = DV.op(lambda e: e.tensor_tensor(v4(d[0]), v4(d[0]), vv[:, :, 0, :], ALU.add), t)
                banks.give(bk, t)
                yield
                t = AC.op(lambda e: e.activation(d[1], d[0], ACT.Abs), t)
                t_e = AC.op(lambda e: e.activation(d[1], d[1], ACT.Exp, scale=-1.0), t)
                yield
                t_w = DV.op(lambda e: e.tensor_scalar(d[2], d[1], 1.0, None, ALU.add), t_e)
                t_w1 = DV.op(lambda e: e.tensor_scalar(d[4], d[2], 1.0, None, ALU.subtract), t_w)
                yield
                t_l = AC.op(lambda e: e.activation(d[3], d[2], ACT.Ln), t_w)
                t = GP.op(lambda e: e.tensor_scalar(d[5], d[4], 0.0, None, ALU.is_equal), t_w1)
                t_g = GP.op(lambda e: e.tensor_tensor(d[5], d[5], d[1], ALU.mult), t)
                yield
                t = DV.op(lambda e: e.tensor_scalar(d[4], d[4], 1e-30, None, ALU.max), t_g)
                t = DV.op(lambda e: e.reciprocal(d[6], d[4]), t)
                t = DV.op(lambda e: e.tensor_tensor(d[6], d[6], d[1], ALU.mult), t)
                t = DV.op(lambda e: e.tensor_tensor(d[6], d[6], d[3], ALU.mult), t, t_l)
                t = DV.op(lambda e: e.tensor_tensor(d[6], d[6], d[5], ALU.add), t)
                t_dt = DV.op(lambda e: e.scalar_tensor_tensor(out=dt, in0=d[0], scalar=0.0, in1=d[6], op0=ALU.max,
                                                              op1=ALU.add), t, *dtt.readers(g))
                tok["dt", g] = t_dt
                t = DV.op(lambda e: e.tensor_tensor(v4(d[7]), v4(dt), bc(negA[:, :]), ALU.mult), t_dt, t_nA)
                yield
                t_a = AC.op(lambda e: e.activation(d[7], d[7], ACT.Exp), t)
                yield
                yield
                bd, free = banks.take()
                t = PE.op(lambda e: e.transpose(bd[0:8 * NB, 0:128], d[7], ident[:, :]), t_a, *free)
                tok["dts"] = [t, t_dt]
                t = DV.op(lambda e: e.tensor_copy(decT[g][:, 1:128], bd[0:8 * NB, 1:128]), t, *decT.readers(g),
                          *t_pad)
                banks.give(bd, t)
                t = dma(f"scr{g % 2}", scratch[g].rearrange("(p t) -> p t", p=8 * NB), decT[g][:, :], t)
                decT.read_by(g, [t])
                tok["scr", g] = t

            ds = steps()
            acc_t = {}
            for i in range(8):
                next(ds, None)
                if i < 6:
                    n, c = g * 6 + i, i
                    bk, free = banks.take()
                    t = project3(bk, (bk, free), (512 + c * 128, 0), g, True)
                    v = bk[:, 0:T].rearrange("p (b t) -> p b t", b=NB)
                    t1 = AC.op(lambda e, v=v, n=n: e.activation(XP[n][:, :, 3:131], v, ACT.Copy), t, *t_pad,
                               *XP.readers(n))
                    t2 = AC.op(lambda e, v=v, n=n, c=c: e.activation(
                        ACC[n][:, :, :], v, ACT.Identity, bias=cw[:, c, 4:5], scale=cw[:, c, 3:4]),
                        t, t_cw2, *ACC.readers(n))
                    banks.give(bk, t2)
                    acc_t[i] = t1, t2
                    yield
                if 1 <= i < 7:
                    n, c = g * 6 + i - 1, i - 1
                    t1, t = acc_t[i - 1]
                    for k in range(3):
                        t = DV.op(lambda e, k=k, n=n, c=c: e.scalar_tensor_tensor(
                            out=ACC[n][:, :, :], in0=XP[n][:, :, k:k + 128], scalar=cw[:, c, k:k + 1],
                            in1=ACC[n][:, :, :], op0=ALU.mult, op1=ALU.add), t, t1, t_cw2)
                    XP.read_by(n, [t])
                    acc_t[i - 1] = t
                    yield
                if i >= 2:
                    n, c = g * 6 + i - 2, i - 2
                    xc = XC[g][:, c, :].rearrange("p (b t) -> p b t", b=NB)
                    t = AC.op(lambda e, n=n, xc=xc: e.activation(xc, ACC[n][:, :, :], ACT.Tanh), acc_t[i - 2],
                              *XC.readers(g))
                    yield
                    t_xc = DV.op(lambda e, n=n, xc=xc: e.scalar_tensor_tensor(
                        out=xc, in0=xc, scalar=1.0, in1=ACC[n][:, :, :], op0=ALU.add, op1=ALU.mult), t)
                    ACC.read_by(n, [t_xc])
                    yield
            for _ in ds:
                yield
            tok["xc", g] = t_xc

        t_db = {}

        def fetch(ns):
            g, b = ns // NB, ns % NB
            t_db[ns] = dma(f"db{ns % 2}", DB[ns][:, :], scratch[g, b * 1024:(b + 1) * 1024].rearrange(
                "(a n) -> a n", a=1).to_broadcast([128, 1024]), tok["scr", g], *DB.readers(ns))

        cv = lambda x: x.rearrange("p (c t) -> p c t", c=4)
        hv = lambda x: x.rearrange("p (h d) -> p h d", h=8)

        def first_half(ns):
            g, b = ns // NB, ns % NB
            t_xc, t_dt = tok["xc", g], tok["dt", g]
            ts = slice(b * 128, (b + 1) * 128)
            if ns not in t_db:
                fetch(ns)
            bx, free = banks.take()
            t_x = turns(bx, lambda i: XC[g][:, i, ts], 0, 4, t_xc, *free)
            t = AC.op(lambda e: e.activation(XH[ns][:, :], bx[:, :], ACT.Copy), t_x, *XH.readers(ns))
            banks.give(bx, t)
            t_dx = GP.op(lambda e: e.tensor_tensor(
                cv(DX[ns][:, :]), XC[g][:, 0:4, ts],
                pc[:, 14:18].unsqueeze(2).to_broadcast([128, 4, 128]), ALU.mult), t_xc, t_pc, *DX.readers(ns))
            t_xd = GP.op(lambda e: e.tensor_tensor(
                hv(XH[ns][:, :]), hv(XH[ns][:, :]),
                dtt[g][:, b * 8:b * 8 + 8].unsqueeze(2).to_broadcast([128, 8, 64]), ALU.mult), t, t_dt)
            t_l = DV.op(lambda e: e.tensor_tensor_scan(
                L[ns][:, :, :].rearrange("p h t -> p (h t)"), DB[ns][:, :],
                id8[:, :, :].rearrange("p h t -> p (h t)"), 0.0, ALU.mult, ALU.add),
                t_db[ns], t_id8, *L.readers(ns))
            DB.read_by(ns, [t_l])
            yield
            bg, free = banks.take()
            t_gm = PE.op(lambda e: e.matmul(bg[:, 0:128], XC[g][:, 4, ts], XC[g][:, 5, ts],
                                            start=True, stop=True), t_xc, *free)
            yield
            t_m = DV.op(lambda e: e.tensor_tensor(
                L[ns][:, :, :], L[ns][:, :, :], bg[:, 0:128].unsqueeze(1).to_broadcast([128, 8, 128]), ALU.mult),
                t_l, t_gm)
            banks.give(bg, t_m)
            if b == NB - 1:
                XC.read_by(g, [t_gm, t_dx])
            yield
            for p in range(2 if b == 0 else 0):
                bz, free = banks.take()
                for i in range(2):
                    t_x = project3(bz, (bz, free), ((2 * p + i) * 128, i * T), g, i == 1)
                sz, z = SZ[g][:, 2 * p:2 * p + 2, :], bz[:, :].rearrange("p (c t) -> p c t", c=2)
                t = AC.op(lambda e, sz=sz, z=z: e.activation(sz, z, ACT.Tanh), t_x, *SZ.readers(g))
                yield
                t_sz = DV.op(lambda e, sz=sz, z=z: e.scalar_tensor_tensor(
                    out=sz, in0=sz, scalar=1.0, in1=z, op0=ALU.add, op1=ALU.mult), t)
                banks.give(bz, t_sz)
                yield
            if b == 0:
                xnT.read_by(g, [t_x])
                xnL.read_by(g, [t_x])
                tok["sz", g] = t_sz
            t_sz = tok["sz", g]
            yield
            yield
            yield
            by, free = banks.take()
            for h in range(8):
                t = PE.op(lambda e, h=h: e.matmul(
                    by[64 * (h % 2):64 * (h % 2) + 64, (h // 2) * 128:(h // 2 + 1) * 128],
                    XH[ns][:, h * 64:h * 64 + 64], L[ns][:, h, :],
                    start=True, stop=True), t_m, t_xd, *free, last=(h == 7))
            L.read_by(ns, [t])
            XH.read_by(ns, [t])
            dtt.read_by(g, [t_xd])
            if ("scr", (ns + 1) // NB) in tok:
                fetch(ns + 1)
            yield
            t = DV.op(lambda e: e.tensor_tensor(Y[ns][:, :], by[:, :], DX[ns][:, :], ALU.add),
                      t, t_dx, *Y.readers(ns))
            DX.read_by(ns, [t])
            banks.give(by, t)
            t = GP.op(lambda e: e.tensor_tensor(cv(Y[ns][:, :]), cv(Y[ns][:, :]), SZ[g][:, :, ts], ALU.mult), t, t_sz)
            SZ.read_by(g, [t])
            tok["y", ns] = t

        def second_half(ns):
            g, b = ns // NB, ns % NB
            st = stb[ns]
            t_y = tok["y", ns]
            t_sq2 = AC.op(lambda e: e.activation(SQ[ns][:, :, :], cv(Y[ns][:, :]), ACT.Square), t_y, *SQ.readers(ns))
            yield
            t = GP.op(lambda e: e.tensor_tensor(SQ[ns][:, 0:2, :], SQ[ns][:, 0:2, :], SQ[ns][:, 2:4, :], ALU.add), t_sq2)
            t_s2 = GP.op(lambda e: e.tensor_tensor(SQ[ns][:, 0, :], SQ[ns][:, 0, :], SQ[ns][:, 1, :], ALU.add), t)
            yield
            bo, free = banks.take()
            for k in range(4):
                PE.op(lambda e, k=k: e.matmul(bo[:, 0:256], Y[ns][:, k * 128:(k + 1) * 128], wout[:, k, :],
                                              start=(k == 0), stop=(k == 3)), t_y, t_wo2, *free, last=False)
            t_o = PE.op(lambda e: e.matmul(bo[:, 256:257], SQ[ns][:, 0, :], ones1[:, :], start=True, stop=True),
                        t_s2, t_one)
            SQ.read_by(ns, [t_o])
            Y.read_by(ns, [t_o])
            t = DV.op(lambda e: e.tensor_scalar(st[:, 1:2], bo[:, 256:257], 1.0 / 512, EPS, ALU.mult, ALU.add),
                      t_o, *stb.readers(ns))
            t_r2 = GP.op(lambda e: e.tensor_tensor(st[:, 1:2], st[:, 1:2], mhalf[:, :], ALU.pow), t, t_mh)
            yield
            hh = X2[g][:, b, :]
            t = DV.op(lambda e: e.scalar_tensor_tensor(
                out=hh, in0=bo[:, 0:256], scalar=st[:, 1:2], in1=X2[g][:, b, :], op0=ALU.mult, op1=ALU.add),
                t_o, t_r2)
            banks.give(bo, t)
            t = layer_stats(hh, st, 2, t)
            yield
            t = DV.op(lambda e: e.tensor_scalar(
                xh[ns][:, :], hh, st[:, 2:3], st[:, 3:4], ALU.subtract, ALU.mult), t, *xh.readers(ns))
            stb.read_by(ns, [t])
            yield
            yield
            hb, free = banks.take()
            t = turns(hb, lambda i: xh[ns][:, i * 128:(i + 1) * 128], 0, 2, t, *free)
            xh.read_by(ns, [t])
            t = AC.op(lambda e: e.activation(HT[g][:, :, b * 128:(b + 1) * 128], hb[:, 0:256].rearrange(
                "p (k t) -> p k t", k=2), ACT.Copy), t, *HT.readers(g))
            banks.give(hb, t)
            tok["h", g] = t

        def stream_b2(g):
            for b in range(NB):
                ns = g * NB + b
                halves = [first_half(ns)] if ns < NG * NB else []
                if ns >= 1 and ns - 1 < NG * NB:
                    halves.append(second_half(ns - 1))
                while halves:
                    for h in list(halves):
                        try:
                            next(h)
                        except StopIteration:
                            halves.remove(h)
                        yield

        qc = [0]

        def stream_c(g):
            t_k1, t_v = tok["ctx", g]
            t_wq1s, t_bq1 = tok["wq1"]
            for m in range(2):
                bk, t = project(wq1, HT[g], m, tok["h", g], t_wq1s)
                t_q = AC.op(lambda e, m=m, bk=bk: e.activation(Q1T[g][:, m, :], bk[:, 0:T], ACT.Identity,
                                                               bias=bq1[:, m:m + 1]), t, t_bq1, *Q1T.readers(g))
                banks.give(bk, t_q)
                yield
            HT.read_by(g, [t])
            exp_t, pt_t = {}, {}
            N = 4
            st = stc[g]
            for i in range(N + LTC + LA):
                if i < N:
                    n = qc[0] + i
                    bk, free = banks.take()
                    r3 = slice(32 * i, 32 * i + 3)
                    r = slice(32 * i, 32 * i + 32)
                    for q in range(4):
                        m, tt = q % 2, slice((q // 2) * 128, (q // 2 + 1) * 128)
                        t_s = PE.op(lambda e, bk=bk, q=q, m=m, tt=tt, r=r: e.matmul(
                            bk[:, q * 128:(q + 1) * 128], Q1T[g][r, m, tt], K1T[g][r, m, tt],
                            start=(q == 0), stop=False), t_q, t_k1, *free, last=False)
                    t_s = PE.op(lambda e, bk=bk, r3=r3: e.matmul(bk[:, :], onesb[r3, :], maskb[r3, :, :].rearrange(
                        "p a k -> p (a k)"), start=False, stop=True), t_mb, t_ones)
                    softmax_part(bk, t_s, PC_, n, st, 1.0, stc.readers(g) if i == 0 else [], 4 * i)
                    t_d = (DV.sem, DV.n)
                    yield
                if LN <= i < N + LN:
                    n = qc[0] + i - LN
                    rc = st[:, 16 + 4 * (i - LN):20 + 4 * (i - LN)]
                    t = DV.op(lambda e, rc=rc: e.reciprocal(rc, rc), exp_t[i - LN])
                    exp_t[i - LN] = GP.op(lambda e, n=n, rc=rc: e.tensor_tensor(
                        PC_[n][:, :, :], PC_[n][:, :, :], rc.unsqueeze(2).to_broadcast([128, 4, 128]), ALU.mult), t)
                    if i == N + LN - 1:
                        stc.read_by(g, [exp_t[i - LN]])
                    yield
                if LTC <= i < N + LTC:
                    n = qc[0] + i - LTC
                    bk, free = banks.take()
                    P = PC_[n]
                    t = turns(bk, lambda q, P=P: P[:, q, :], 0, 4, exp_t[i - LTC], *free)
                    PC_.read_by(n, [t])
                    t = AC.op(lambda e, bk=bk, n=n: e.activation(PTC[n][:, :, :], bk[:, :].rearrange(
                        "p (i k) -> p i k", i=4), ACT.Copy), t, *PTC.readers(n))
                    banks.give(bk, t)
                    pt_t[i - LTC] = t
                    yield
                if i < N:
                    for q in range(4):
                        exp_t[i] = AC.op(lambda e, n=qc[0] + i, q=q, i=i: e.activation(
                            PC_[n][:, q, :], PC_[n][:, q, :], ACT.Exp, scale=32 ** -0.5,
                            accum_out=st[:, 16 + 4 * i + q:17 + 4 * i + q]), t_d)
                if i >= LTC + LA and (i - LTC - LA) % 2 == 1:
                    k = (i - LTC - LA) // 2
                    if k == 0:
                        o, free = banks.take()
                    for b in range(NB):
                        for m in range(2):
                            for j in (2 * k, 2 * k + 1):
                                c = 2 * m + j % 2
                                t_o = PE.op(lambda e, o=o, b=b, k=k, c=c, n=qc[0] + j, m=m: e.matmul(
                                    o[32 * c:32 * c + 32, (2 * b + k) * 128:(2 * b + k + 1) * 128],
                                    V1[g][:, b, 4 * k + c, :], PTC[n][:, 2 * b + m, :], start=True, stop=True),
                                    pt_t[j], t_v, *free, last=(b == 1 and c == 3))
                    for j in (2 * k, 2 * k + 1):
                        PTC.read_by(qc[0] + j, [t_o])
                    yield
            t_ot = AC.op(lambda e, o=o: e.activation(OT[g][:, :, :], o[:, :].rearrange("p (k t) -> p k t", k=4),
                                                     ACT.Copy), t_o, *OT.readers(g))
            banks.give(o, t_ot)
            yield
            yield
            bo, free = banks.take()
            for b in range(NB):
                for k in range(2):
                    t = PE.op(lambda e, bo=bo, b=b, k=k: e.matmul(
                        bo[:, b * 256:(b + 1) * 256], OT[g][:, 2 * b + k, :], wo[:, k, :],
                        start=(k == 0), stop=(k == 1)), t_ot, t_wo, *free, last=(b == 1 and k == 1))
            OT.read_by(g, [t])
            yield
            t_h = DV.op(lambda e, bo=bo: e.tensor_tensor(
                X2[g][:, :, :], bo[:, :].rearrange("p (b c) -> p b c", b=NB), X2[g][:, :, :], ALU.add), t)
            banks.give(bo, t_h)
            X2.read_by(g, [dma(f"out{g % 2}", a["out"][g], X2[g][:, :, :], t_h)])
            yield
            K1T.read_by(g, [t_s])
            Q1T.read_by(g, [t_s])
            V1.read_by(g, [t_o])
            qc[0] += N

        lags = ((stream_a1, 0, NG), (stream_a2, 1, NG), (stream_b1, 2, NG), (stream_b2, 3, NG + 1), (stream_c, 5, NG),
                (stream_k, 4, NG))
        for step in range(NG + 5):
            if step == 2:
                setup_wq1()
            merge([f(step - lag) if 0 <= step - lag < n else None for f, lag, n in lags], SHARE, PHASE)
        SP.wait([(rec[0], rec[1]) for rec in dma_sems.values()])

        block = ctx.enter_context(nc.Block())
        block.tensor(PE.run)
        block.vector(DV.run)
        block.scalar(AC.run)
        block.gpsimd(GP.run)
        block.sync(SP.run)


def kernel(x, ctx_1024, mask_BxS2_ik0, mask_1xS2_bf0, **w):
    import numpy as np
    import concourse.bacc as bacc
    from concourse.bass_utils import run_bass_kernel_spmd

    w = {k: np.asarray(v) for k, v in w.items()}
    x, c = np.asarray(x), np.asarray(ctx_1024)

    def feature_major(v):
        return np.ascontiguousarray(v.reshape(NG, T, 2, 128).transpose(0, 3, 2, 1))

    def rows(v):
        return np.ascontiguousarray(v.reshape(-1, 128, v.shape[-1]).transpose(1, 0, 2))

    def cols(v):
        return v.reshape(-1, 128).T

    p = np.arange(128)
    pcols = np.zeros((128, 20), np.float32)
    for at, n, name in ((4, 2, "L1_xattn_m_norm_w"),
                        (6, 4, "L1_xattn_gnorm_w"), (10, 2, "L1_xattn_ca_ln_w"), (12, 2, "L1_xattn_ca_ln_b")):
        pcols[:, at:at + n] = cols(w[name])
    pcols[:, 14:18] = cols(np.repeat(w["L1_xattn_D_skip"], 64))
    order = np.concatenate([16 * (4 * j + 2 * m + e) + np.arange(16)
                            for m in range(2) for j in range(4) for e in range(2)])
    pcols[:, 0:2], pcols[:, 2:4] = cols(w["L0_xattn_bq"][order]), cols(w["L0_xattn_bk"][order])
    order1 = np.concatenate([32 * (4 * k + 2 * m + i) + np.arange(32)
                             for m in range(2) for k in range(2) for i in range(2)])
    arrays = {
        "ident": np.eye(128, dtype=np.float32),
        "par": np.stack([(p // 16 + 1) % 2, (p // 16) % 2], 1).astype(np.float32),
        "sel": np.stack([p % 32 == i for i in range(3)], 1).astype(np.float32),
        "pcols": pcols,
        "convp": np.ascontiguousarray(np.concatenate(
            [w["L1_xattn_conv_w"].reshape(6, 128, 4), w["L1_xattn_conv_b"].reshape(6, 128, 1)], 2).transpose(1, 0, 2)),
        "heads": np.concatenate([w["L1_xattn_dt_bias"], w["L1_xattn_A_log"]])[None],
        "maskT": np.ascontiguousarray(np.asarray(mask_BxS2_ik0).T),
        "pad": np.asarray(mask_1xS2_bf0),
        "xT": feature_major(x), "cT": feature_major(c),
        "xt": np.ascontiguousarray(x.reshape(NG, NB, S, D).transpose(0, 2, 1, 3)),
        "wq": rows(w["L0_xattn_Wq"][:, order]), "wk": rows(w["L0_xattn_Wk"][:, order]),
        "wv": rows(w["L0_xattn_Wv"]), "wv1": rows(w["L1_xattn_Wv"]),
        "wk1": rows(w["L1_xattn_Wk"][:, order1]), "wq1": rows(w["L1_xattn_Wq"][:, order1]), "wo": rows(w["L1_xattn_Wo"]),
        "win": rows(w["L1_xattn_in_proj_w"]), "wout": rows(w["L1_xattn_out_proj_w"]),
        "bv": w["L0_xattn_bv"], "gamma": w["L0_xattn_gamma"], "beta": w["L0_xattn_beta"],
    }
    nc = bacc.Bacc("TRN2", target_bir_lowering=False, num_devices=1)
    args, ins = {}, {}
    for name, v in arrays.items():
        ins["in_" + name] = v
        args[name] = nc.dram_tensor("in_" + name, v.shape, mybir.dt.from_np(v.dtype), kind="ExternalInput").ap()
    args["out"] = nc.dram_tensor("out_x", (NG, S, NB, D), F32, kind="ExternalOutput").ap()
    program(nc, args)
    r = run_bass_kernel_spmd(nc, [ins], core_ids=[0])
    out = r.results[0]["out_x"]
    return np.ascontiguousarray(out.transpose(0, 2, 1, 3)).reshape(NG * NB, S, D)
```
